# Optimizing a Trainium2 kernel written in Bass

```python
import numpy as np
import jax
import jax.numpy as jnp

def _softmax(x, axis=-1):
    return jax.nn.softmax(x, axis=axis)

def _gelu(x):
    return jax.nn.gelu(x, approximate=True)

def _silu(x):
    return jax.nn.silu(x)

def _sigmoid(x):
    return jax.nn.sigmoid(x)

def _layernorm(x, axis=-1, eps=1e-05):
    m = jnp.mean(x, axis=axis, keepdims=True)
    v = jnp.var(x, axis=axis, keepdims=True)
    return (x - m) / jnp.sqrt(v + eps)

def _scatter_add(tgt, idx, src, axis=0):
    return tgt.at[idx].add(src)

def _segment_sum(src, seg, n):
    return jax.ops.segment_sum(src, seg, n)
kernel_name = 'mk_lm_tower_d1_tok_ids512_r4_e1dd5a'

def setup_inputs(seed: int=0):
    np.random.seed(seed)
    _w = jnp.asarray

    def _rec_inputs():
        import jax
        import jax.numpy as jnp
        _rk = jax.random.key(seed)
        x = jax.random.randint(jax.random.fold_in(_rk, 1), (16, 256), 0, 10000, jnp.int32)
        return x
    x = _rec_inputs()

    def _L0_tok_setup():
        import jax, jax.numpy as jnp
        import numpy as np
        B, S, H = (64, 512, 128)
        VOCAB = 10000

        def _syntax_info(token_ids):
            t = token_ids
            opens = (t == 40) | (t == 123) | (t == 91)
            closes = (t == 41) | (t == 125) | (t == 93)
            delta = opens.astype(jnp.int32) - closes.astype(jnp.int32)
            s = jnp.cumsum(delta, axis=1)
            run_min = jax.lax.cummin(s, axis=1)
            nesting = jnp.clip(s - jnp.minimum(run_min, 0), 0, 15)
            segments = jnp.cumsum((t > 39990).astype(jnp.int32), axis=1) % 8
            return (nesting, segments)
        key = jax.random.key(seed)
        k1, k2, k3, k4, k5 = jax.random.split(key, 5)
        token_ids = jax.random.randint(k1, (B, S), 0, VOCAB, dtype=jnp.int64) if jax.config.jax_enable_x64 else jax.random.randint(k1, (B, S), 0, VOCAB, dtype=jnp.int32)
        std = 0.02
        pos_table = jax.random.normal(k2, (S, H), dtype=jnp.float32) * std
        nest_table = jax.random.normal(k3, (16, H), dtype=jnp.float32) * std
        seg_table = jax.random.normal(k4, (8, H), dtype=jnp.float32) * std
        W = jax.random.normal(k5, (3 * H, H), dtype=jnp.float32) * (1.0 / np.sqrt(3 * H))
        return {'token_ids': token_ids, 'pos_table': pos_table, 'nest_table': nest_table, 'seg_table': seg_table, 'W': W}
    _L0_tok_all = _L0_tok_setup()
    _L0_tok_in = {k: v for k, v in _L0_tok_all.items() if k in ('pos_table', 'nest_table', 'seg_table', 'W')}
    del _L0_tok_all

    def _L0_attn_setup():
        import jax, jax.numpy as jnp
        import numpy as np
        B, N, DIM = (4, 1024, 128)
        H, DH = (8, 64)
        F = 64
        CS = 128

        def _kernel_fn(t, proj):
            tp = jnp.einsum('...d,fd->...f', t, proj)
            return jnp.exp(tp - jnp.max(tp, axis=-1, keepdims=True))
        key = jax.random.key(seed)
        k1, k2, k3, k4 = jax.random.split(key, 4)
        x = jax.random.normal(k1, (B, N, DIM), jnp.float32)
        w_qkv = jax.random.normal(k2, (3 * H * DH, DIM), jnp.float32) / jnp.sqrt(DIM)
        w_out = jax.random.normal(k3, (DIM, H * DH), jnp.float32) / jnp.sqrt(H * DH)
        b_out = jnp.zeros((DIM,), jnp.float32)
        proj = jnp.linalg.qr(jax.random.normal(k4, (F, DH), jnp.float32))[0]
        return {'x': x, 'w_qkv': w_qkv, 'w_out': w_out, 'b_out': b_out, 'proj': proj}
    _L0_attn_all = _L0_attn_setup()
    _L0_attn_in = {k: v for k, v in _L0_attn_all.items() if k in ('w_qkv', 'w_out', 'b_out', 'proj')}
    del _L0_attn_all

    def _L0_ffn_setup():
        import jax, jax.numpy as jnp
        import numpy as np
        B, T, D, FF, E = (4, 512, 128, 512, 8)
        TOP_K = 2
        EPS = 0.01
        key = jax.random.key(seed)
        ks = jax.random.split(key, 7)
        s = 0.02
        return {'x': jax.random.normal(ks[0], (B, T, D), dtype=jnp.float32), 'Wg': jax.random.normal(ks[1], (D, E), dtype=jnp.float32) * s, 'bg': jnp.zeros((E,), dtype=jnp.float32), 'W1': jax.random.normal(ks[2], (E, D, FF), dtype=jnp.float32) * s, 'b1': jnp.zeros((E, FF), dtype=jnp.float32), 'W2': jax.random.normal(ks[3], (E, FF, D), dtype=jnp.float32) * s, 'b2': jnp.zeros((E, D), dtype=jnp.float32)}
    _L0_ffn_all = _L0_ffn_setup()
    _L0_ffn_in = {k: v for k, v in _L0_ffn_all.items() if k in ('Wg', 'bg', 'W1', 'b1', 'W2', 'b2')}
    del _L0_ffn_all
    return {'x': x, 'L0_tok_pos_table': _L0_tok_in['pos_table'], 'L0_tok_nest_table': _L0_tok_in['nest_table'], 'L0_tok_seg_table': _L0_tok_in['seg_table'], 'L0_tok_W': _L0_tok_in['W'], 'L0_attn_w_qkv': _L0_attn_in['w_qkv'], 'L0_attn_w_out': _L0_attn_in['w_out'], 'L0_attn_b_out': _L0_attn_in['b_out'], 'L0_attn_proj': _L0_attn_in['proj'], 'L0_ffn_Wg': _L0_ffn_in['Wg'], 'L0_ffn_bg': _L0_ffn_in['bg'], 'L0_ffn_W1': _L0_ffn_in['W1'], 'L0_ffn_b1': _L0_ffn_in['b1'], 'L0_ffn_W2': _L0_ffn_in['W2'], 'L0_ffn_b2': _L0_ffn_in['b2']}

def reference(x, L0_tok_pos_table, L0_tok_nest_table, L0_tok_seg_table, L0_tok_W, L0_attn_w_qkv, L0_attn_w_out, L0_attn_b_out, L0_attn_proj, L0_ffn_Wg, L0_ffn_bg, L0_ffn_W1, L0_ffn_b1, L0_ffn_W2, L0_ffn_b2):
    import jax
    import jax.numpy as jnp

    def _L0_tok_ref(token_ids, pos_table, nest_table, seg_table, W):
        import jax, jax.numpy as jnp
        import numpy as np
        B, S, H = (64, 512, 128)
        VOCAB = 10000

        def _syntax_info(token_ids):
            t = token_ids
            opens = (t == 40) | (t == 123) | (t == 91)
            closes = (t == 41) | (t == 125) | (t == 93)
            delta = opens.astype(jnp.int32) - closes.astype(jnp.int32)
            s = jnp.cumsum(delta, axis=1)
            run_min = jax.lax.cummin(s, axis=1)
            nesting = jnp.clip(s - jnp.minimum(run_min, 0), 0, 15)
            segments = jnp.cumsum((t > 39990).astype(jnp.int32), axis=1) % 8
            return (nesting, segments)
        b, s = token_ids.shape
        positions = jnp.arange(s)
        pos_emb = jnp.broadcast_to(pos_table[positions][None], (b, s, pos_table.shape[-1]))
        nesting, segments = _syntax_info(token_ids)
        nest_emb = nest_table[nesting]
        seg_emb = seg_table[segments]
        combined = jnp.concatenate([pos_emb, nest_emb, seg_emb], axis=-1)
        return jnp.einsum('bsk,kh->bsh', combined, W)

    def _L0_attn_ref(x, w_qkv, w_out, b_out, proj):
        import jax, jax.numpy as jnp
        import numpy as np
        B, N, DIM = (4, 1024, 128)
        H, DH = (8, 64)
        F = 64
        CS = 128

        def _kernel_fn(t, proj):
            tp = jnp.einsum('...d,fd->...f', t, proj)
            return jnp.exp(tp - jnp.max(tp, axis=-1, keepdims=True))
        b, n, _ = x.shape
        scale = DH ** (-0.5)
        c = n // CS
        qkv = x @ w_qkv.T
        q, k, v = jnp.split(qkv, 3, axis=-1)

        def to_chunks(t):
            return t.reshape(b, n, H, DH).transpose(0, 2, 1, 3).reshape(b, H, c, CS, DH)
        q = to_chunks(q) * scale
        k = to_chunks(k)
        v = to_chunks(v)
        q_prime = _kernel_fn(q, proj)
        k_prime = _kernel_fn(k, proj)
        k_sum = k_prime.sum(axis=3)
        D = jnp.einsum('bhcsf,bhcf->bhcs', q_prime, k_sum)
        D_inv = 1.0 / (D + 0.0001)
        context = jnp.einsum('bhcsf,bhcsd->bhcfd', k_prime, v)
        out = jnp.einsum('bhcsf,bhcfd->bhcsd', q_prime, context)
        out = out * D_inv[..., None]
        out = out.reshape(b, H, n, DH).transpose(0, 2, 1, 3).reshape(b, n, H * DH)
        return out @ w_out.T + b_out

    def _L0_ffn_ref(x, Wg, bg, W1, b1, W2, b2):
        import jax, jax.numpy as jnp
        import numpy as np
        B, T, D, FF, E = (4, 512, 128, 512, 8)
        TOP_K = 2
        EPS = 0.01
        b, t, d = x.shape
        e = Wg.shape[1]
        logits = jnp.einsum('btd,de->bte', x, Wg) + bg
        gates = jax.nn.softmax(logits, axis=-1)
        vals, idx = jax.lax.top_k(gates, TOP_K)
        vals = vals / (jnp.sum(vals, axis=-1, keepdims=True) + EPS)
        w = jnp.sum(jax.nn.one_hot(idx, e, dtype=x.dtype) * vals[..., None], axis=-2)
        w = w.reshape(-1, e)
        xf = x.reshape(-1, d)
        h = jax.nn.relu(jnp.einsum('nd,edf->enf', xf, W1) + b1[:, None, :])
        y = jnp.einsum('enf,efd->end', h, W2) + b2[:, None, :]
        out = jnp.einsum('ne,end->nd', w, y)
        return out.reshape(b, t, d)
    h = _L0_tok_ref(x, L0_tok_pos_table, L0_tok_nest_table, L0_tok_seg_table, L0_tok_W)
    h = h + _L0_attn_ref(_layernorm(h, axis=-1), L0_attn_w_qkv, L0_attn_w_out, L0_attn_b_out, L0_attn_proj)
    h = h + _L0_ffn_ref(_layernorm(h, axis=-1), L0_ffn_Wg, L0_ffn_bg, L0_ffn_W1, L0_ffn_b1, L0_ffn_W2, L0_ffn_b2)
    return h

_drawn_inputs = setup_inputs


def setup_inputs(seed=0):
    import zlib

    import numpy as np

    out = dict(_drawn_inputs(seed))
    spreads = {'L0_attn_b_out': (0.0, 0.1),
     'L0_ffn_bg': (0.0, 0.323),
     'L0_ffn_b1': (0.0, 0.355),
     'L0_ffn_b2': (0.0, 0.1)}
    factors = {}
    for name, (base, spread) in spreads.items():
        noise = np.random.default_rng([zlib.crc32(name.encode()), seed]).standard_normal(out[name].shape)
        drawn = base * np.exp(spread * noise) if base else spread * noise
        out[name] = jnp.asarray(drawn.astype(out[name].dtype))
    for name, factor in factors.items():
        out[name] = (out[name] * factor).astype(out[name].dtype)
    return out
```

```python
from contextlib import ExitStack

import concourse.bass as bass
from concourse import mybir


class Steps:

    def __init__(self, eng, sem):
        self.eng, self.sem, self.base, self.count = eng, sem, 0, 0

    def done(self, instruction):
        self.add(instruction)
        self.eng.wait_ge(self.sem, self.base + self.count)

    def add(self, instruction):
        instruction.then_inc(self.sem, 1)
        self.count += 1


def span(start, size):
    return slice(start, start + size) if isinstance(start, int) else bass.ds(start, size)


def lm_tower_kernel(nc, x, pos_table, nest_table, seg_table, tok_w, w_qkv, w_out, b_out, proj,
                    w_gate, b_gate, w_one, b_one, w_two, b_two, out):
    f32 = mybir.dt.float32
    f32r = mybir.dt.float32r
    bf16 = mybir.dt.bfloat16
    i32 = mybir.dt.int32
    ALU = mybir.AluOpType
    ACT = mybir.ActivationFunctionType
    AX = mybir.AxisListType

    B, S = x.shape
    P = 128
    D = tok_w.shape[1]
    PAIRS = B
    TILES = B * S // P
    HEADS, DH = 8, 64
    HC = HEADS // 2
    HD = HEADS * DH
    NNEST, NSEG = nest_table.shape[0], seg_table.shape[0]
    E = w_gate.shape[1]
    FF = w_one.shape[2]
    FC = FF // P
    LN_EPS, D_EPS, TOP_EPS = 1e-5, 1e-4, 0.01
    BIG = 3.0e38
    SLOT = 32
    PARTS = 3
    TR = SLOT * PARTS
    GROUPS = B * S // 512

    ctx = ExitStack()
    with ctx:
        def sb(name, shape, dt=f32):
            return ctx.enter_context(nc.sbuf_tensor(name, shape, dt))

        def pb(name, shape):
            return ctx.enter_context(nc.psum_tensor(name, shape, f32))

        def sem(name):
            return ctx.enter_context(nc.semaphore(name))

        ident = sb("ident", [P, P])
        minus_half = sb("minus_half", [P, 2])
        ln_eps = sb("ln_eps", [P, 2])
        spare = sb("spare", [P, 2])
        priority = sb("priority", [P, TILES, E])
        table_id = sb("table_id", [TR, 1])
        tok_rows = sb("tok_rows", [P, 3, D])
        pos_rows = sb("pos_rows", [P, 2, D])
        nest_rows = sb("nest_rows", [TR, D])
        seg_rows = sb("seg_rows", [TR, D])
        proj_diag = sb("proj_diag", [P, P])
        qkv_rows = sb("qkv_rows", [P, 3 * HC, D])
        out_rows = sb("out_rows", [P, HD])
        b1_rows = sb("b1_rows", [E * FC, P])
        gate_w = sb("gate_w", [P, E])
        gate_b = sb("gate_b", [P, E])
        out_b = sb("out_b", [P, D])
        b2_all = sb("b2_all", [P, E, D])
        w1_all = sb("w1_all", [P, E, FF])
        w2_all = sb("w2_all", [P, E, FC, D])
        pos_nest_seg_T = sb("pos_nest_seg_T", [P, 2 * P + 2 * TR])
        proj_T = sb("proj_T", [P, P])
        b1_T = sb("b1_T", [P, E * FC])
        out_w = sb("out_w", [P, HC, D])
        pos_part = sb("pos_part", [P, 2, D])
        part_hi = sb("part_hi", [TR, D], bf16)
        part_mid = sb("part_mid", [TR, D], bf16)
        part_lo = sb("part_lo", [TR, D], bf16)
        rest_one = sb("rest_one", [TR, D])
        rest_two = sb("rest_two", [TR, D])
        table = sb("table", [TR, D], bf16)
        qkv_hi = sb("qkv_hi", [P, 3, HD], f32r)
        qkv_lo = sb("qkv_lo", [P, 3, HD], f32r)

        tokens = sb("tokens", [B, S], i32)
        zeros = sb("zeros", [B, S])
        delta = sb("delta", [B, S])
        other = sb("other", [B, S])
        depth = sb("depth", [B, S])
        floor = sb("floor", [B, S])
        nesting = sb("nesting", [B, S], bf16)
        seg_count = sb("seg_count", [B, S], i32)
        seg_int = sb("seg_int", [B, S], i32)
        segments = sb("segments", [B, S], bf16)
        row_of = sb("row_of", [TR, B * S], bf16)
        one_hot = sb("one_hot", [TR, 2, S], bf16)

        h = sb("h", [P, 2, 2, D])
        h_bias = sb("h_bias", [P, 2, 2, D])
        stats = sb("stats", [P, 2, 6])
        moments = sb("moments", [P, 2, 2, 2])
        rstd = sb("rstd", [P, 2, 2])
        xhat = sb("xhat", [P, 2, 2, D])
        xT_hi = sb("xT_hi", [P, 2, S], f32r)
        xT_lo = sb("xT_lo", [P, 2, S], f32r)

        qk_max = sb("qk_max", [P, 2, HEADS])
        q_prime = sb("q_prime", [P, 2, HD])
        k_prime = sb("k_prime", [P, 2, HD])
        v_ones = sb("v_ones", [P, 2, HEADS, DH + 1])
        context = sb("context", [P, 2, HC, DH + 1])
        qT = sb("qT", [P, 2, HC, P])
        d_inv = sb("d_inv", [P, 2, HC])
        d_sum = sb("d_sum", [P, 2, HC])
        heads_out = sb("heads_out", [P, 2, HD])
        oT = sb("oT", [P, 2, HC, P])
        h2 = sb("h2", [P, 2, 2, D])

        stats2 = sb("stats2", [P, 2, 6])
        moments2 = sb("moments2", [P, 2, 2, 2])
        rstd2 = sb("rstd2", [P, 2, 2])
        xhat2 = sb("xhat2", [P, 2, 2, D])
        x2T = sb("x2T", [P, 2, S])
        h2_all = sb("h2_all", [P, TILES, D])
        x2T_all = sb("x2T_all", [P, B * S])
        logits = sb("logits", [P, TILES, E])
        gate = [sb(f"gate{i}", [P, TILES, E]) for i in range(7)]
        col = [sb(f"col{i}", [P, TILES]) for i in range(8)]
        hT = sb("hT", [P, 2, FC, 512])
        y_b = sb("y_b", [P, 4, D])
        total = sb("total", [P, 2, 4, D])

        ps_q = pb("ps_q", [P, HD])
        ps_k = pb("ps_k", [P, HD])
        ps_vc = pb("ps_vc", [P, HD])
        ps_qT = pb("ps_qT", [P, HD])
        ps_out = pb("ps_out", [P, 2, HD])
        ps_oy = pb("ps_oy", [P, HD])
        ps_ln = pb("ps_ln", [P, HD])
        ps_ctx = ps_vc[:, 0:HC * (DH + 1)].rearrange("p (c d) -> p c d", c=HC)

        ids_dram = nc.dram_tensor("ids_dram", [2, B, S], bf16)

        s_tok = sem("tokens_in")
        s_emb_w = sem("embedding_weights_in")
        s_att_w = sem("attention_weights_in")
        s_ffn_w = sem("ffn_weights_in")
        s_zero = sem("tables_zeroed")
        s_ident = sem("ident_made")
        s_const = sem("constants_made")
        s_vec = sem("vector_chain")
        s_pool = sem("pool_chain")
        s_ids = sem("ids_made")
        s_ids_out = sem("ids_in_dram")
        s_row = sem("rows_in")
        s_t1 = sem("setup_transposed")
        s_t1c = sem("setup_copied")
        s_wT = sem("weight_products")
        s_wTc = sem("weight_products_split")
        s_hi = sem("weight_highs")

        s_hot = sem("one_hot_ready")
        s_emb = sem("embedding_done")
        s_h = sem("h_ready")
        s_mom = sem("moments_ready")
        s_xhat = sem("xhat_ready")
        s_hb = sem("h_bias_ready")
        s_xT = sem("xT_done")
        s_xh = sem("xT_hi_ready")
        s_xl = sem("xT_lo_ready")
        s_q, s_k, s_v = sem("q_done"), sem("k_done"), sem("v_done")
        s_qs, s_ks = sem("q_shifted"), sem("k_shifted")
        s_qp, s_kp, s_vo = sem("q_prime_ready"), sem("k_prime_ready"), sem("v_ready")
        s_c, s_cr = sem("context_done"), sem("context_ready")
        s_qT, s_qTr = sem("qT_done"), sem("qT_ready")
        s_o, s_or = sem("out_done"), sem("heads_out_ready")
        s_oT, s_oTr = sem("oT_done"), sem("oT_ready")
        s_y, s_h2 = sem("y_done"), sem("h2_ready")
        s_mom2, s_xhat2 = sem("moments2_ready"), sem("xhat2_ready")
        s_x2T, s_x2Tr = sem("x2T_done"), sem("x2T_ready")
        s_lg, s_lgr = sem("logits_done"), sem("logits_ready")
        s_kept_h2 = [sem(f"h2_kept{a}") for a in range(2)]
        s_kept_x2T = [sem(f"x2T_kept{a}") for a in range(2)]
        s_gd, s_ge = sem("gate_diffs"), sem("gate_exps")
        s_w = sem("gates_ready")
        s_f1, s_f1a, s_f1d = sem("hidden_done"), sem("hidden_by_act"), sem("hidden_by_dve")
        s_f2, s_f2r, s_tot = sem("experts_out"), sem("experts_read"), sem("total_ready")
        s_out = [sem(f"out_written{a}") for a in range(2)]

        block = ctx.enter_context(nc.Block())

        EMB_DMAS = 8
        ATT_DMAS = 5
        FFN_DMAS = 7

        @block.sync
        def _(sp):
            sp.dma_start(tokens[:, :], x[:, :]).then_inc(s_tok, 16)
            sp.dma_start(tok_rows[:, :, :], tok_w.rearrange("(a p) h -> p a h", p=P)).then_inc(s_emb_w, 16)
            sp.dma_start(pos_rows[:, :, :], pos_table[0:S, :].rearrange("(a p) h -> p a h", p=P)).then_inc(s_emb_w, 16)
            sp.wait_ge(s_zero, 1)
            for r in range(PARTS):
                sp.dma_start(nest_rows[SLOT * r:SLOT * r + NNEST, :], nest_table[:, :]).then_inc(s_emb_w, 16)
                sp.dma_start(seg_rows[SLOT * r + NNEST:SLOT * r + NNEST + NSEG, :], seg_table[:, :]).then_inc(s_emb_w, 16)
            for r in range(2):
                sp.dma_start(proj_diag[DH * r:DH * r + DH, DH * r:DH * r + DH], proj[:, :]).then_inc(s_att_w, 16)
            sp.wait_ge(s_ids, 1)
            sp.dma_start(ids_dram[0, :, :], nesting[:, :]).then_inc(s_ids_out, 16)
            sp.wait_ge(s_ids, 2)
            sp.dma_start(ids_dram[1, :, :], segments[:, :]).then_inc(s_ids_out, 16)
            sp.wait_ge(s_ids_out, 32)
            for r in range(2 * PARTS):
                sp.dma_start(row_of[16 * r:16 * r + 16, :],
                             ids_dram[r % 2, :, :].rearrange("(o b) s -> o (b s)", o=1).to_broadcast([16, B * S]))\
                    .then_inc(s_row, 16)
            sp.dma_start(b1_rows[:, :], b_one.rearrange("e (c p) -> (e c) p", p=P)).then_inc(s_ffn_w, 16)
            sp.dma_start(w1_all[:, :, :], w_one.rearrange("e d f -> d e f")).then_inc(s_ffn_w, 16)
            sp.dma_start(w2_all[:, :, :, :], w_two.rearrange("e (c p) d -> p e c d", p=P)).then_inc(s_ffn_w, 16)

            def keep(p, a):
                sp.wait_ge(s_h2, 2 * p + 2)
                sp.dma_start(h2_all[:, bass.ds(2 * p, 2), :], h2[:, a, :, :]).then_inc(s_kept_h2[a], 16)
                sp.wait_ge(s_x2Tr, p + 1)
                sp.dma_start(x2T_all[:, bass.ds(p * S, S)], x2T[:, a, :]).then_inc(s_kept_x2T[a], 16)

            with sp.Fori(0, PAIRS // 2) as i:
                for a in range(2):
                    keep(2 * i + a, a)
            with sp.Fori(0, GROUPS // 2) as i:
                for a in range(2):
                    g = 2 * i + a
                    sp.wait_ge(s_tot, g + 1)
                    sp.dma_start(out.rearrange("b s d -> (b s) d")[bass.ds(g * 512, 512), :]
                                 .rearrange("(j p) d -> p j d", p=P), total[:, a, :, :]).then_inc(s_out[a], 16)
            for a in range(2):
                sp.wait_ge(s_out[a], 16 * GROUPS // 2)

        @block.gpsimd
        def _(pool):
            step = Steps(pool, s_pool)
            nc.gpsimd.memset(nest_rows[:, :], 0.0)
            nc.gpsimd.memset(seg_rows[:, :], 0.0)
            nc.gpsimd.memset(proj_diag[:, :], 0.0).then_inc(s_zero, 1)
            step.done(nc.gpsimd.memset(ident[:, :], 0.0))
            nc.gpsimd.affine_select(out=ident[:, :], in_=ident[:, :], compare_op=ALU.not_equal, fill=1.0, base=0,
                                    pattern=[[-1, P]], channel_multiplier=1).then_inc(s_ident, 1)
            nc.gpsimd.memset(minus_half[:, :], -0.5)
            nc.gpsimd.memset(ln_eps[:, :], LN_EPS)
            for a in range(2):
                step.done(nc.gpsimd.memset(v_ones[:, a, :, DH:DH + 1], 1.0))
            for r in range(PARTS):
                step.done(nc.gpsimd.iota(table_id[SLOT * r:SLOT * r + SLOT, :], [[0, 1]], base=0, channel_multiplier=1,
                                         allow_small_or_imprecise_dtypes=True))
            nc.gpsimd.iota(priority[:, :, :], [[0, TILES], [-1, E]], base=E, channel_multiplier=0,
                           allow_small_or_imprecise_dtypes=True).then_inc(s_const, 1)

            def norm(p, a, mom, rs, src, dst, mom_sem, out_sem, free_sem, first):
                pool.wait_ge(mom_sem, p + 1)
                step.done(nc.gpsimd.tensor_tensor(rs[:, a, :], mom[:, a, :, 1], ln_eps[:, :], ALU.add))
                step.done(nc.gpsimd.tensor_tensor(rs[:, a, :], rs[:, a, :], minus_half[:, :], ALU.pow))
                if not first:
                    pool.wait_ge(free_sem, p - 1)
                nc.gpsimd.tensor_tensor(spare[:, :], minus_half[:, :], ln_eps[:, :], ALU.add)
                for j in range(2):
                    last = nc.gpsimd.tensor_scalar(dst[:, a, j, :], src[:, a, j, :], mom[:, a, j, 0:1],
                                                   rs[:, a, j:j + 1], ALU.subtract, ALU.mult)
                last.then_inc(out_sem, 1)

            def norm_one(p, a, first=False):
                norm(p, a, moments, rstd, h, xhat, s_mom, s_xhat, s_xT, first)
                if not first:
                    pool.wait_ge(s_h2, 2 * p - 2)
                nc.gpsimd.tensor_tensor(h_bias[:, a, :, :], h[:, a, :, :],
                                        out_b[:, None, :].to_broadcast([P, 2, D]), ALU.add).then_inc(s_hb, 1)

            def norm_two(p, a, first=False):
                norm(p, a, moments2, rstd2, h2, xhat2, s_mom2, s_xhat2, s_x2T, first)

            pool.wait_ge(s_att_w, 16 * ATT_DMAS)
            norm_one(0, 0, True)
            norm_one(1, 1, True)
            norm_two(0, 0, True)
            norm_one(2, 0)
            norm_two(1, 1, True)
            step.base, step.count = step.count, 0
            start = step.base
            with pool.Fori(0, (PAIRS - 4) // 2) as i:
                step.base, step.count = start + i * 8, 0
                norm_one(2 * i + 3, 1)
                norm_two(2 * i + 2, 0)
                norm_one(2 * i + 4, 0)
                norm_two(2 * i + 3, 1)
            step.base, step.count = start + 8 * ((PAIRS - 4) // 2), 0
            norm_one(PAIRS - 1, 1)
            norm_two(PAIRS - 2, 0)
            norm_two(PAIRS - 1, 1)

        @block.scalar
        def _(act):
            act.dma_start(qkv_rows[:, :, :], w_qkv.rearrange("(a p) c -> p a c", p=P)).then_inc(s_att_w, 16)
            act.dma_start(out_rows[:, :], w_out[:, :]).then_inc(s_att_w, 16)
            act.dma_start(out_b[:, :], b_out.rearrange("(o d) -> o d", o=1).to_broadcast([P, D])).then_inc(s_att_w, 16)
            act.dma_start(gate_w[:, :], w_gate[:, :]).then_inc(s_ffn_w, 16)
            act.dma_start(gate_b[:, :], b_gate.rearrange("(o d) -> o d", o=1).to_broadcast([P, E])).then_inc(s_ffn_w, 16)
            act.dma_start(b2_all[:, :, :], b_two.rearrange("(o e) d -> o e d", o=1).to_broadcast([P, E, D])).then_inc(s_ffn_w, 16)
            act.wait_ge(s_t1, 1)
            nc.scalar.activation(pos_nest_seg_T[:, :], ps_q[:, 0:2 * P + 2 * TR], ACT.Copy).then_inc(s_t1c, 1)
            act.wait_ge(s_t1, 2)
            nc.scalar.activation(proj_T[:, :], ps_k[:, 0:P], ACT.Copy).then_inc(s_t1c, 1)
            act.wait_ge(s_t1, 3)
            nc.scalar.activation(out_w[:, :, :], ps_qT[:, :], ACT.Copy).then_inc(s_hi, 1)
            act.wait_ge(s_t1, 4)
            nc.scalar.activation(qkv_hi[:, 2, :], ps_vc[:, :], ACT.Copy).then_inc(s_hi, 1)
            act.wait_ge(s_wT, 2)
            nc.scalar.activation(qkv_hi[:, 0, :], ps_out[:, 0, :], ACT.Copy, scale=DH ** -0.5).then_inc(s_hi, 1)
            act.wait_ge(s_wT, 3)
            nc.scalar.activation(qkv_hi[:, 1, :], ps_out[:, 1, :], ACT.Copy).then_inc(s_hi, 1)
            act.wait_ge(s_t1, 5)
            nc.scalar.activation(b1_T[:, :], ps_oy[:, 0:E * FC], ACT.Copy).then_inc(s_hi, 1)

            def xT_high(p, a, first=False):
                act.wait_ge(s_xT, p + 1)
                if not first:
                    act.wait_ge(s_v, 2 * p - 2)
                nc.scalar.activation(xT_hi[:, a, :], ps_ln[:, 0:S], ACT.Copy).then_inc(s_xh, 1)

            def q_exp(t, a):
                act.wait_ge(s_qs, t + 1)
                nc.scalar.activation(q_prime[:, a, :], q_prime[:, a, :], ACT.Exp).then_inc(s_qp, 1)

            def k_exp(t, a):
                act.wait_ge(s_ks, t + 1)
                nc.scalar.activation(k_prime[:, a, :], k_prime[:, a, :], ACT.Exp).then_inc(s_kp, 1)

            def v_copy(t, a, first=False):
                act.wait_ge(s_v, t + 1)
                if not first:
                    act.wait_ge(s_c, t - 1)
                nc.scalar.activation(v_ones[:, a, :, 0:DH], ps_vc[:, :].rearrange("p (h d) -> p h d", h=HEADS),
                                     ACT.Copy).then_inc(s_vo, 1)

            def qT_copy(t, a, first=False):
                act.wait_ge(s_qT, t + 1)
                if not first:
                    act.wait_ge(s_o, t - 1)
                nc.scalar.activation(qT[:, a, :, :], ps_qT[:, :], ACT.Copy).then_inc(s_qTr, 1)

            def context_copy(t, a):
                act.wait_ge(s_c, t + 1)
                nc.scalar.activation(context[:, a, :, :], ps_ctx, ACT.Copy).then_inc(s_cr, 1)

            def oT_copy(t, a):
                act.wait_ge(s_oT, t + 1)
                nc.scalar.activation(oT[:, a, :, :], ps_oy[:, :], ACT.Copy).then_inc(s_oTr, 1)

            def x2T_copy(p, a, half, first=False):
                act.wait_ge(s_x2T, p + 1)
                if not first:
                    act.wait_ge(s_kept_x2T[a], 16 * half)
                nc.scalar.activation(x2T[:, a, :], ps_ln[:, 0:S], ACT.Copy).then_inc(s_x2Tr, 1)

            def pair(p, a, half, head=False, last=False):
                for j in range(2):
                    t = 2 * p + j
                    more = not (last and j == 1)
                    context_copy(t, j)
                    if more:
                        q_exp(t + 1, 1 - j)
                    if j == 0 and not last:
                        xT_high(p + 1, 1 - a, head)
                    if j == 1 and not head:
                        x2T_copy(p - 1, 1 - a, half - 1 if a == 0 else half, isinstance(p, int) and p - 1 < 2)
                    if more:
                        k_exp(t + 1, 1 - j)
                        v_copy(t + 1, 1 - j, head and j == 0)
                    oT_copy(t, j)
                    if more:
                        qT_copy(t + 1, 1 - j, head and j == 0)

            act.wait_ge(s_const, 1)
            xT_high(0, 0, True)
            q_exp(0, 0)
            k_exp(0, 0)
            v_copy(0, 0, True)
            qT_copy(0, 0, True)
            pair(0, 0, 0, head=True)
            pair(1, 1, 0)
            pair(2, 0, 1)
            pair(3, 1, 1)
            with act.Fori(0, (PAIRS - 6) // 2) as i:
                pair(2 * i + 4, 0, i + 2)
                pair(2 * i + 5, 1, i + 2)
            pair(PAIRS - 2, 0, PAIRS // 2 - 1)
            pair(PAIRS - 1, 1, PAIRS // 2 - 1, last=True)
            x2T_copy(PAIRS - 1, 1, PAIRS // 2 - 1)

            act.wait_ge(s_gd, 1)
            nc.scalar.activation(gate[2][:, :, :], gate[1][:, :, :], ACT.Exp).then_inc(s_ge, 1)
            act.wait_ge(s_gd, 2)
            nc.scalar.activation(col[3][:, :], col[2][:, :], ACT.Exp).then_inc(s_ge, 1)

            banks = [ps_q, ps_k, ps_vc, ps_qT]
            def feed_forward(g):
                for e in range(E):
                    for c in range(0, FC, 2):
                        n = g * (E * FC) + e * FC + c
                        act.wait_ge(s_f1, n + 1)
                        nc.scalar.activation(hT[:, e % 2, c, :], banks[c][:, :], ACT.Relu,
                                             bias=b1_T[:, e * FC + c:e * FC + c + 1]).then_inc(s_f1a, 1)

            feed_forward(0)
            with act.Fori(1, GROUPS) as g:
                feed_forward(g)

        @block.vector
        def _(dve):
            step = Steps(dve, s_vec)
            step.done(nc.vector.memset(zeros[:, :], 0.0))
            dve.wait_ge(s_tok, 16)
            step.done(nc.vector.tensor_scalar(delta[:, :], tokens[:, :], 40, None, ALU.is_equal))
            for code, op in ((123, ALU.add), (91, ALU.add)):
                step.done(nc.vector.scalar_tensor_tensor(delta[:, :], tokens[:, :], code, delta[:, :], ALU.is_equal, op))
            step.done(nc.vector.tensor_scalar(other[:, :], tokens[:, :], 41, None, ALU.is_equal))
            for code in (125, 93):
                step.done(nc.vector.scalar_tensor_tensor(other[:, :], tokens[:, :], code, other[:, :],
                                                         ALU.is_equal, ALU.add))
            step.done(nc.vector.tensor_tensor(delta[:, :], delta[:, :], other[:, :], ALU.subtract))
            step.done(nc.vector.tensor_tensor_scan(depth[:, :], delta[:, :], zeros[:, :], 0.0, ALU.add, ALU.add))
            step.done(nc.vector.tensor_tensor_scan(floor[:, :], depth[:, :], zeros[:, :], 0.0, ALU.min, ALU.min))
            step.done(nc.vector.tensor_tensor(depth[:, :], depth[:, :], floor[:, :], ALU.subtract))
            nc.vector.tensor_scalar(nesting[:, :], depth[:, :], float(NNEST - 1), 0.0, ALU.min, ALU.max).then_inc(s_ids, 1)
            step.done(nc.vector.tensor_scalar(other[:, :], tokens[:, :], 39990, None, ALU.is_gt))
            step.done(nc.vector.tensor_tensor_scan(seg_count[:, :], other[:, :], zeros[:, :], 0.0, ALU.add, ALU.add))
            step.done(nc.vector.tensor_scalar(seg_int[:, :], seg_count[:, :], NSEG - 1, None, ALU.bitwise_and))
            dve.wait_ge(s_const, 1)
            nc.vector.tensor_scalar(segments[:, :], seg_int[:, :], float(NNEST), None, ALU.add).then_inc(s_ids, 1)

            dve.wait_ge(s_wT, 1)
            step.done(nc.vector.tensor_copy(pos_part[:, :, :], ps_oy[:, 0:2 * D].rearrange("p (a d) -> p a d", a=2)))
            tab = ps_oy[0:TR, 2 * D:3 * D]
            step.done(nc.vector.tensor_copy(part_hi[:, :], tab))
            step.done(nc.vector.tensor_tensor(rest_one[:, :], tab, part_hi[:, :], ALU.subtract))
            step.done(nc.vector.tensor_copy(part_mid[:, :], rest_one[:, :]))
            step.done(nc.vector.tensor_tensor(rest_two[:, :], rest_one[:, :], part_mid[:, :], ALU.subtract))
            step.done(nc.vector.tensor_copy(part_lo[:, :], rest_two[:, :]))
            for r, part in enumerate((part_hi, part_mid, part_lo)):
                last = nc.vector.tensor_copy(table[SLOT * r:SLOT * r + SLOT, :], part[SLOT * r:SLOT * r + SLOT, :])
            last.then_inc(s_wTc, 1)
            dve.wait_ge(s_hi, 2)
            nc.vector.tensor_tensor(qkv_lo[:, 2, :], ps_vc[:, :], qkv_hi[:, 2, :].bitcast(f32), ALU.subtract)
            dve.wait_ge(s_hi, 3)
            nc.vector.scalar_tensor_tensor(qkv_lo[:, 0, :], ps_out[:, 0, :], DH ** -0.5, qkv_hi[:, 0, :].bitcast(f32),
                                           ALU.mult, ALU.subtract)
            dve.wait_ge(s_hi, 4)
            nc.vector.tensor_tensor(qkv_lo[:, 1, :], ps_out[:, 1, :], qkv_hi[:, 1, :].bitcast(f32),
                                    ALU.subtract).then_inc(s_wTc, 1)

            def hot(p, a, first=False):
                if not first:
                    dve.wait_ge(s_emb, p - 1)
                nc.vector.tensor_scalar(one_hot[:, a, :], row_of[:, bass.ds(p * S, S)] if not isinstance(p, int)
                                        else row_of[:, p * S:p * S + S], table_id[:, 0:1], None,
                                        ALU.is_equal).then_inc(s_hot, 1)

            def stats_of(a, src, st):
                for j in range(2):
                    last = nc.vector.bn_stats(st[:, j, :], src[:, a, j, :])
                step.add(last)

            def moments_of(a, st, mom, out_sem):
                for j in range(2):
                    last = nc.vector.bn_aggr(mom[:, a, j, :], st[:, j, :])
                last.then_inc(out_sem, 1)

            def embed(p, a, first=False):
                dve.wait_ge(s_emb, p + 1)
                if not first:
                    dve.wait_ge(s_hb, p - 1)
                ins = nc.vector.tensor_tensor(h[:, a, :, :], ps_ln[:, 0:S].rearrange("p (a d) -> p a d", a=2),
                                              pos_part[:, :, :], ALU.add)
                ins.then_inc(s_h, 1)
                dve.wait_ge(s_h, p + 1)
                stats_of(a, h, stats)

            def xT_low(p, a):
                dve.wait_ge(s_xh, p + 1)
                nc.vector.tensor_tensor(xT_lo[:, a, :], ps_ln[:, 0:S], xT_hi[:, a, :].bitcast(f32),
                                        ALU.subtract).then_inc(s_xl, 1)

            def shift(t, a, ps, dst, n, done_sem, free_sem, out_sem, first):
                heads = ps[:, :].rearrange("p (h f) -> p h f", h=HEADS)
                dve.wait_ge(done_sem, t + 1)
                step.done(nc.vector.tensor_reduce(qk_max[:, n, :], heads, AX.X, ALU.max))
                if not first:
                    dve.wait_ge(free_sem, t - 1)
                nc.vector.tensor_tensor(dst[:, a, :].rearrange("p (h f) -> p h f", h=HEADS), heads,
                                        qk_max[:, n, :, None].to_broadcast([P, HEADS, DH]),
                                        ALU.subtract).then_inc(out_sem, 1)

            def q_shift(t, a, first=False):
                shift(t, a, ps_q, q_prime, 0, s_q, s_qT, s_qs, first)

            def k_shift(t, a, first=False):
                shift(t, a, ps_k, k_prime, 1, s_k, s_c, s_ks, first)

            def normalize(t, a):
                dve.wait_ge(s_o, t + 1)
                heads = ps_out[:, :, 0:HC * (DH + 1)].rearrange("p r (c d) -> p r c d", c=HC)
                step.done(nc.vector.tensor_scalar(d_sum[:, :, :], heads[:, :, :, DH], D_EPS, None, ALU.add))
                step.done(nc.vector.reciprocal(d_inv[:, :, :], d_sum[:, :, :]))
                for r in range(2):
                    last = nc.vector.tensor_tensor(
                        heads_out[:, a, :].rearrange("p (c r d) -> p r c d", c=HC, r=2)[:, r],
                        heads[:, r, :, 0:DH], d_inv[:, r, :, None].to_broadcast([P, HC, DH]), ALU.mult)
                last.then_inc(s_or, 1)

            def residual(t, a, j, p):
                dve.wait_ge(s_y, t + 1)
                dve.wait_ge(s_hb, p + 1)
                nc.vector.tensor_tensor(h2[:, a, j, :], ps_oy[:, 0:D], h_bias[:, a, j, :], ALU.add).then_inc(s_h2, 1)

            def gate_logits(p):
                dve.wait_ge(s_lg, p + 1)
                at = bass.ds(2 * p, 2) if not isinstance(p, int) else slice(2 * p, 2 * p + 2)
                nc.vector.tensor_tensor(logits[:, at, :], ps_ln[:, 0:2 * E].rearrange("p (j e) -> p j e", j=2),
                                        gate_b[:, None, :].to_broadcast([P, 2, E]), ALU.add).then_inc(s_lgr, 1)

            def pair(p, a, half, head=False, second=False, last=False, tail=False):
                for j in range(2):
                    t = 2 * p + j
                    more = not (last and j == 1)
                    if j == 0 and not last:
                        embed(p + 1, 1 - a, head)
                    if more:
                        q_shift(t + 1, 1 - j, head and j == 0)
                    if j == 0 and not last:
                        moments_of(1 - a, stats, moments, s_mom)
                    if j == 0 and not head:
                        moments_of(1 - a, stats2, moments2, s_mom2)
                    normalize(t, j)
                    if more:
                        k_shift(t + 1, 1 - j, head and j == 0)
                    if j == 0 and not last:
                        xT_low(p + 1, 1 - a)
                        if not tail:
                            hot(p + 2, a)
                    if j == 1 and not head:
                        gate_logits(p - 1)
                    if j == 0 and not (head or second):
                        dve.wait_ge(s_kept_h2[a], 16 * half)
                        dve.wait_ge(s_xhat2, p - 1)
                    residual(t, a, j, p)
                dve.wait_ge(s_h2, 2 * p + 2)
                stats_of(a, h2, stats2)
                if last:
                    step.done(nc.vector.tensor_copy(col[0][:, 0:1], priority[:, 0, 0:1]))
                    moments_of(a, stats2, moments2, s_mom2)

            dve.wait_ge(s_row, 16 * 2 * PARTS)
            hot(0, 0, True)
            hot(1, 1, True)
            embed(0, 0, True)
            step.done(nc.vector.tensor_copy(col[0][:, 0:1], priority[:, 0, 0:1]))
            moments_of(0, stats, moments, s_mom)
            xT_low(0, 0)
            q_shift(0, 0, True)
            k_shift(0, 0, True)
            dve.wait_ge(s_ffn_w, 16 * 6)
            pair(0, 0, 0, head=True)
            pair(1, 1, 0, second=True)
            start = step.count
            per = 2 * 10
            with dve.Fori(0, (PAIRS - 4) // 2) as i:
                step.base, step.count = start + i * per, 0
                pair(2 * i + 2, 0, i + 1)
                pair(2 * i + 3, 1, i + 1)
                assert step.count == per, step.count
            step.base, step.count = start + per * ((PAIRS - 4) // 2), 0
            pair(PAIRS - 2, 0, PAIRS // 2 - 1, tail=True)
            pair(PAIRS - 1, 1, PAIRS // 2 - 1, last=True)
            gate_logits(PAIRS - 1)
            dve.wait_ge(s_lgr, PAIRS)

            l, d, ex, eq, hot1, d2, hot2 = (g[:, :, :] for g in gate)
            wide = lambda c: c[:, :, None].to_broadcast([P, TILES, E])
            m1, p1, m2, e2, z, den, w2c, p2 = (c[:, :] for c in col)
            lg = logits[:, :, :]
            pri = priority[:, :, :]
            step.done(nc.vector.tensor_reduce(m1, lg, AX.X, ALU.max))
            nc.vector.tensor_tensor(d, lg, wide(m1), ALU.subtract).then_inc(s_gd, 1)
            dve.wait_ge(s_gd, 1)
            step.done(nc.vector.scalar_tensor_tensor(eq, d, 0.0, pri, ALU.is_equal, ALU.mult))
            step.done(nc.vector.tensor_reduce(p1, eq, AX.X, ALU.max))
            step.done(nc.vector.tensor_tensor(hot1, eq, wide(p1), ALU.is_equal))
            step.done(nc.vector.scalar_tensor_tensor(d2, hot1, -BIG, d, ALU.mult, ALU.add))
            nc.vector.tensor_reduce(m2, d2, AX.X, ALU.max).then_inc(s_gd, 1)
            dve.wait_ge(s_gd, 2)
            step.done(nc.vector.tensor_tensor(l, d2, wide(m2), ALU.is_equal))
            step.done(nc.vector.tensor_tensor(l, l, pri, ALU.mult))
            step.done(nc.vector.tensor_reduce(p2, l, AX.X, ALU.max))
            step.done(nc.vector.tensor_tensor(hot2, l, wide(p2), ALU.is_equal))
            dve.wait_ge(s_ge, 2)
            step.done(nc.vector.tensor_reduce(z, ex, AX.X, ALU.add))
            step.done(nc.vector.scalar_tensor_tensor(den, z, TOP_EPS, e2, ALU.mult, ALU.add))
            step.done(nc.vector.tensor_scalar(den, den, 1.0, None, ALU.add))
            step.done(nc.vector.reciprocal(p1, den))
            step.done(nc.vector.tensor_tensor(w2c, e2, p1, ALU.mult))
            step.done(nc.vector.tensor_tensor(hot1, hot1, wide(p1), ALU.mult))
            step.done(nc.vector.tensor_tensor(hot2, hot2, wide(w2c), ALU.mult))
            step.done(nc.vector.tensor_tensor(l, hot1, hot2, ALU.add))
            gates = gate[0]

            banks = [ps_q, ps_k, ps_vc, ps_qT]
            dve.wait_ge(s_ffn_w, 16 * 6)
            start = step.base + step.count
            per = E * 5
            def feed_forward(i):
                for a in range(2):
                    g = 2 * i + a
                    step.base, step.count = start + g * per, 0
                    if not isinstance(i, int):
                        dve.wait_ge(s_out[a], 16 * i)

                    def relu(e):
                        for c in range(1, FC, 2):
                            dve.wait_ge(s_f1, g * (E * FC) + e * FC + c + 1)
                            nc.vector.tensor_scalar(hT[:, e % 2, c, :], banks[c][:, :],
                                                    b1_T[:, e * FC + c:e * FC + c + 1], 0.0, ALU.add,
                                                    ALU.max).then_inc(s_f1d, 1)

                    relu(0)
                    for e in range(E):
                        if e + 1 < E:
                            relu(e + 1)
                        dve.wait_ge(s_f2, g * E + e + 1)
                        ins = nc.vector.tensor_tensor(
                            y_b[:, :, :], ps_out[:, e % 2, :].rearrange("p (j d) -> p j d", j=4),
                            b2_all[:, e, None, :].to_broadcast([P, 4, D]), ALU.add)
                        ins.then_inc(s_f2r, 1)
                        dve.wait_ge(s_f2r, g * E + e + 1)
                        for j in range(4):
                            src = (h2_all[:, span(4 * g + j, 1), :].rearrange("p o d -> p (o d)") if e == 0
                                   else total[:, a, j, :])
                            last = nc.vector.scalar_tensor_tensor(
                                total[:, a, j, :], y_b[:, j, :],
                                gates[:, span(4 * g + j, 1), e], src, ALU.mult, ALU.add)
                            if j == 3:
                                step.count += 4
                            last.then_inc(s_vec, 1)
                        step.count += 1
                        ins = nc.vector.tensor_copy(col[0][:, 0:1], col[1][:, 0:1])
                        ins.then_inc(s_vec, 1)
                        dve.wait_ge(s_vec, step.base + step.count)
                    ins = nc.vector.tensor_copy(col[0][:, 1:2], col[1][:, 1:2])
                    ins.then_inc(s_tot, 1)

            feed_forward(0)
            with dve.Fori(1, GROUPS // 2) as i:
                feed_forward(i)

        @block.tensor
        def _(pe):
            pe.wait_ge(s_ident, 1)
            pe.wait_ge(s_emb_w, 16 * EMB_DMAS)
            idn = ident[:, :]
            for a in range(2):
                nc.tensor.transpose(ps_q[:, a * P:a * P + P], pos_rows[:, a, :], idn)
            nc.tensor.transpose(ps_q[:, 2 * P:2 * P + TR], nest_rows[:, :], ident[0:TR, 0:TR])
            nc.tensor.transpose(ps_q[:, 2 * P + TR:2 * P + 2 * TR], seg_rows[:, :], ident[0:TR, 0:TR]).then_inc(s_t1, 1)
            pe.wait_ge(s_att_w, 16 * ATT_DMAS)
            nc.tensor.transpose(ps_k[:, 0:P], proj_diag[:, :], idn).then_inc(s_t1, 1)
            for c in range(HC):
                last = nc.tensor.transpose(ps_qT[:, c * P:c * P + P], out_rows[:, c * P:c * P + P], idn)
            last.then_inc(s_t1, 1)
            for c in range(HC):
                last = nc.tensor.transpose(ps_vc[:, c * P:c * P + P], qkv_rows[:, 2 * HC + c, :], idn)
            last.then_inc(s_t1, 1)
            pe.wait_ge(s_t1c, 1)
            for a in range(2):
                nc.tensor.matmul(ps_oy[:, a * D:a * D + D], pos_nest_seg_T[:, a * P:a * P + P], tok_rows[:, 0, :],
                                 start=True, stop=True)
            nc.tensor.matmul(ps_oy[0:TR, 2 * D:3 * D], pos_nest_seg_T[:, 2 * P:2 * P + TR], tok_rows[:, 1, :],
                             start=True, stop=False)
            nc.tensor.matmul(ps_oy[0:TR, 2 * D:3 * D], pos_nest_seg_T[:, 2 * P + TR:2 * P + 2 * TR], tok_rows[:, 2, :],
                             start=False, stop=True).then_inc(s_wT, 1)
            pe.wait_ge(s_t1c, 2)
            for n in range(2):
                for c in range(HC):
                    last = nc.tensor.matmul(ps_out[:, n, c * P:c * P + P], qkv_rows[:, n * HC + c, :], proj_T[:, :],
                                            start=True, stop=True)
                last.then_inc(s_wT, 1)
            pe.wait_ge(s_wTc, 1)
            pe.wait_ge(s_ffn_w, 16 * 6)
            nc.tensor.transpose(ps_oy[:, 0:E * FC], b1_rows[:, :], ident[0:E * FC, 0:E * FC]).then_inc(s_t1, 1)
            pe.wait_ge(s_wTc, 2)
            pe.wait_ge(s_hi, 5)

            def embed(p, a, first=False):
                pe.wait_ge(s_hot, p + 1)
                if not first:
                    pe.wait_ge(s_lgr, p - 2)
                for j in range(2):
                    last = nc.tensor.matmul(ps_ln[:, j * D:j * D + D], one_hot[:, a, j * P:j * P + P], table[:, :],
                                            start=True, stop=True)
                last.then_inc(s_emb, 1)

            def x_transpose(p, a):
                pe.wait_ge(s_xhat, p + 1)
                for j in range(2):
                    last = nc.tensor.transpose(ps_ln[:, j * P:j * P + P], xhat[:, a, j, :], idn)
                last.then_inc(s_xT, 1)

            def product(n, ps, a, j, out_sem):
                for m, (w, xt) in enumerate(((qkv_hi, xT_hi), (qkv_lo, xT_hi), (qkv_hi, xT_lo))):
                    last = nc.tensor.matmul(ps[:, :], xt[:, a, j * P:j * P + P], w[:, n, :], start=(m == 0), stop=(m == 2))
                last.then_inc(out_sem, 1)

            def q_product(t, p, a, j):
                pe.wait_ge(s_xl, p + 1)
                pe.wait_ge(s_qs, t)
                product(0, ps_q, a, j, s_q)

            def k_product(t, a, j):
                pe.wait_ge(s_ks, t)
                product(1, ps_k, a, j, s_k)

            def v_product(t, a, j):
                pe.wait_ge(s_cr, t)
                product(2, ps_vc, a, j, s_v)

            def q_transpose(t, a):
                pe.wait_ge(s_qp, t + 1)
                pe.wait_ge(s_qTr, t)
                for c in range(HC):
                    last = nc.tensor.transpose(ps_qT[:, c * P:c * P + P], q_prime[:, a, c * P:c * P + P], idn)
                last.then_inc(s_qT, 1)

            def context_product(t, a):
                pe.wait_ge(s_kp, t + 1)
                pe.wait_ge(s_vo, t + 1)
                for n in range(HEADS):
                    r = DH * (n % 2)
                    last = nc.tensor.matmul(ps_ctx[r:r + DH, n // 2, :], k_prime[:, a, n * DH:n * DH + DH],
                                            v_ones[:, a, n, :], start=True, stop=True)
                last.then_inc(s_c, 1)

            def out_product(t, a):
                pe.wait_ge(s_cr, t + 1)
                pe.wait_ge(s_qTr, t + 1)
                pe.wait_ge(s_or, t)
                for n in range(HEADS):
                    r = DH * (n % 2)
                    c = n // 2
                    last = nc.tensor.matmul(ps_out[:, n % 2, c * (DH + 1):c * (DH + 1) + DH + 1],
                                            qT[r:r + DH, a, c, :], context[r:r + DH, a, c, :], start=True, stop=True)
                last.then_inc(s_o, 1)

            def o_transpose(t, a):
                pe.wait_ge(s_or, t + 1)
                pe.wait_ge(s_h2, t)
                for c in range(HC):
                    last = nc.tensor.transpose(ps_oy[:, c * P:c * P + P], heads_out[:, a, c * P:c * P + P], idn)
                last.then_inc(s_oT, 1)

            def y_product(t, a):
                pe.wait_ge(s_oTr, t + 1)
                for c in range(HC):
                    last = nc.tensor.matmul(ps_oy[:, 0:D], oT[:, a, c, :], out_w[:, c, :], start=(c == 0), stop=(c == HC - 1))
                last.then_inc(s_y, 1)

            def x2_transpose(p, a):
                pe.wait_ge(s_xhat2, p + 1)
                for j in range(2):
                    last = nc.tensor.transpose(ps_ln[:, j * P:j * P + P], xhat2[:, a, j, :], idn)
                last.then_inc(s_x2T, 1)

            def gate_product(p, a):
                pe.wait_ge(s_x2Tr, p + 1)
                for j in range(2):
                    last = nc.tensor.matmul(ps_ln[:, j * E:j * E + E], x2T[:, a, j * P:j * P + P], gate_w[:, :],
                                            start=True, stop=True)
                last.then_inc(s_lg, 1)

            def pair(p, a, head=False, last=False):
                for j in range(2):
                    t = 2 * p + j
                    nt, na, nj = (p, a, 1) if j == 0 else (p + 1, 1 - a, 0)
                    more = not (last and j == 1)
                    if j == 0 and not last:
                        embed(p + 1, 1 - a, head)
                    context_product(t, j)
                    if more:
                        q_product(t + 1, nt, na, nj)
                    out_product(t, j)
                    if more:
                        k_product(t + 1, na, nj)
                    if j == 0 and not last:
                        x_transpose(p + 1, 1 - a)
                    if j == 1 and not head:
                        pe.wait_ge(s_xl, p + (0 if last else 1) + 1)
                        x2_transpose(p - 1, 1 - a)
                    if more:
                        v_product(t + 1, na, nj)
                    o_transpose(t, j)
                    if more:
                        q_transpose(t + 1, 1 - j)
                    if j == 1 and not head:
                        gate_product(p - 1, 1 - a)
                    y_product(t, j)

            embed(0, 0, True)
            x_transpose(0, 0)
            q_product(0, 0, 0, 0)
            k_product(0, 0, 0)
            v_product(0, 0, 0)
            q_transpose(0, 0)
            pe.wait_ge(s_xl, 1)
            pair(0, 0, head=True)
            def second_pair():
                pair(1, 1)
            second_pair()
            with pe.Fori(0, (PAIRS - 4) // 2) as i:
                pair(2 * i + 2, 0)
                pair(2 * i + 3, 1)
            pair(PAIRS - 2, 0)
            pair(PAIRS - 1, 1, last=True)
            pe.wait_ge(s_lgr, PAIRS - 1)
            x2_transpose(PAIRS - 1, 1)
            gate_product(PAIRS - 1, 1)
            pe.wait_ge(s_ffn_w, 16 * (FFN_DMAS - 1))
            for a in range(2):
                pe.wait_ge(s_kept_x2T[a], 16 * PAIRS // 2)

            banks = [ps_q, ps_k, ps_vc, ps_qT]
            def feed_forward(g):
                def wait_up(sem, e, c):
                    n = g * (E * FC // 2) + 2 * e + c // 2 - 1
                    if not isinstance(n, int) or n > 0:
                        pe.wait_ge(sem, n)

                def up(e):
                    for c in range(FC):
                        if c % 2 == 0:
                            wait_up(s_f1a, e, c)
                        else:
                            wait_up(s_f1d, e, c)
                        nc.tensor.matmul(banks[c][:, :], w1_all[:, e, c * P:c * P + P],
                                         x2T_all[:, span(g * 512, 512)], start=True, stop=True).then_inc(s_f1, 1)

                def down(e):
                    pe.wait_ge(s_f1a, g * 16 + 2 * e + 2)
                    pe.wait_ge(s_f1d, g * 16 + 2 * e + 2)
                    if not isinstance(g, int) or e > 1:
                        pe.wait_ge(s_f2r, g * E + e - 1)
                    for j in range(4):
                        for c in range(FC):
                            last = nc.tensor.matmul(ps_out[:, e % 2, j * D:j * D + D], hT[:, e % 2, c, j * P:j * P + P],
                                                    w2_all[:, e, c, :], start=(c == 0), stop=(c == FC - 1))
                    last.then_inc(s_f2, 1)

                up(0)
                for e in range(E):
                    if e + 1 < E:
                        up(e + 1)
                    down(e)

            feed_forward(0)
            with pe.Fori(1, GROUPS) as g:
                feed_forward(g)


_INS = ['x', 'L0_tok_pos_table', 'L0_tok_nest_table', 'L0_tok_seg_table', 'L0_tok_W', 'L0_attn_w_qkv',
        'L0_attn_w_out', 'L0_attn_b_out', 'L0_attn_proj', 'L0_ffn_Wg', 'L0_ffn_bg', 'L0_ffn_W1', 'L0_ffn_b1',
        'L0_ffn_W2', 'L0_ffn_b2']
_OUT = (16, 256, 128)


def kernel(**inputs):
    import numpy as _np
    import concourse.bacc as _bacc
    from concourse import mybir as _mybir
    from concourse.bass_utils import run_bass_kernel_spmd as _run

    nc = _bacc.Bacc("TRN2", target_bir_lowering=False, num_devices=1)
    arrays, args = {}, []
    for name in _INS:
        a = _np.ascontiguousarray(inputs[name])
        arrays[f"in_{name}"] = a
        args.append(nc.dram_tensor(f"in_{name}", a.shape, _mybir.dt.from_np(a.dtype), kind="ExternalInput").ap())
    args.append(nc.dram_tensor("out", _OUT, _mybir.dt.float32, kind="ExternalOutput").ap())
    lm_tower_kernel(nc, *args)
    r = _run(nc, [arrays], core_ids=[0])
    return r.results[0]["out"]
```

```python
from contextlib import ExitStack

import concourse.bass as bass
from concourse import mybir


class Steps:

    def __init__(self, eng, sem):
        self.eng, self.sem, self.base, self.count = eng, sem, 0, 0

    def done(self, instruction):
        self.add(instruction)
        self.wait()

    def add(self, instruction):
        instruction.then_inc(self.sem, 1)
        self.count += 1

    def wait(self):
        self.eng.wait_ge(self.sem, self.base + self.count)


def span(start, size):
    return slice(start, start + size) if isinstance(start, int) else bass.ds(start, size)


def wait(eng, sem, count):
    if not isinstance(count, int) or count > 0:
        eng.wait_ge(sem, count)


def lm_tower_kernel(nc, x, pos_table, nest_table, seg_table, tok_w, w_qkv, w_out, b_out, proj,
                    w_gate, b_gate, w_one, b_one, w_two, b_two, out):
    f32 = mybir.dt.float32
    f32r = mybir.dt.float32r
    bf16 = mybir.dt.bfloat16
    i32 = mybir.dt.int32
    u32 = mybir.dt.uint32
    ALU = mybir.AluOpType
    ACT = mybir.ActivationFunctionType
    AX = mybir.AxisListType

    B, S = x.shape
    P = 128
    D = tok_w.shape[1]
    SEQS = B
    TILES = B * S // P
    HEADS, DH = 8, 64
    HC = HEADS // 2
    HD = HEADS * DH
    NNEST, NSEG = nest_table.shape[0], seg_table.shape[0]
    E = w_gate.shape[1]
    E_BITS = (E - 1).bit_length()
    FF = w_one.shape[2]
    FC = FF // P
    TOP = 2
    LN_EPS, D_EPS, TOP_EPS = 1e-5, 1e-4, 0.01
    SLOT = 32
    PARTS = 3
    TR = SLOT * PARTS

    CHOICES = TOP * B * S
    CAP = B * S + P
    FTILES = CHOICES // P + E
    EMPTY = E * CAP
    EMPTIES = FTILES - CHOICES // P
    SLOTS = EMPTY + EMPTIES * P
    ROW = D + 2 * E
    PLACES = CHOICES + E * P + EMPTIES * P

    L0, L1 = 4, SEQS - 2
    AHEAD = 5
    RING = 6

    def live(n, count=SEQS):
        return not isinstance(n, int) or 0 <= n < count

    def sequences(eng, step, body, per=None):
        for p in range(-2, L0):
            body(p, p % 2, p // 2)
        start = step.base + step.count if step else 0
        with eng.Fori(0, (L1 - L0) // 2) as i:
            if step:
                step.base, step.count = start + i * per, 0
            for a in range(2):
                body(2 * i + L0 + a, a, i + L0 // 2)
            if step:
                assert step.count == per, step.count
        if step:
            step.base, step.count = start + per * ((L1 - L0) // 2), 0
        for p in range(L1, SEQS + 3):
            body(p, p % 2, p // 2)

    def slot_tiles(eng, body, step=None, per=None, groups=None):
        def load(group):
            if groups is None:
                return [None] * (RING + 2)
            word = eng.value_load(groups[0:1, span(group, 1)], min_val=0, max_val=E ** (RING + 2) - 1)
            return [eng.snap((word >> (E_BITS * k)) & (E - 1)) for k in range(RING + 2)]

        values = load(0)
        for n in range(-2, RING):
            body(n, n % RING, n // RING, values[max(n, 0)], values[n + 2])
        start = step.base + step.count if step else 0
        with eng.Fori(1, FTILES // RING - 1) as i:
            values = load(i)
            if step:
                step.base, step.count = start + (i - 1) * per, 0
            for a in range(RING):
                body(i * RING + a, a, i, values[a], values[a + 2])
            if step:
                assert step.count == per, step.count
        if step:
            step.base, step.count = start + per * (FTILES // RING - 2), 0
        first = FTILES - RING
        values = load(FTILES // RING - 1)
        for n in range(first, FTILES + 2):
            body(n, n % RING, n // RING, values[n - first], values[min(n - first + 2, RING + 1)])

    ctx = ExitStack()
    with ctx:
        def sb(name, shape, dt=f32):
            return ctx.enter_context(nc.sbuf_tensor(name, shape, dt))

        def pb(name, shape):
            return ctx.enter_context(nc.psum_tensor(name, shape, f32))

        def sem(name):
            return ctx.enter_context(nc.semaphore(name))

        ident = sb("ident", [P, P])
        before = sb("before", [P, P], bf16)
        ones = sb("ones", [P, P], bf16)
        part_ones = sb("part_ones", [TR, P], bf16)
        minus_half = sb("minus_half", [P, 2])
        ln_eps = sb("ln_eps", [P, 2])
        spare = sb("spare", [P, 2])
        zero = sb("zero", [P, 2])
        one = sb("one", [P, 2])
        minus_one = sb("minus_one", [P, 2])
        top_eps = sb("top_eps", [P, 2])
        second = sb("second", [P, E])
        table_id = sb("table_id", [TR, 1])
        expert_id = sb("expert_id", [P, E])
        expert_at = sb("expert_at", [P, E + 1])
        token_id = sb("token_id", [P, TILES])
        tile_id = sb("tile_id", [P, FTILES])
        pad_rows = sb("pad_rows", [P, E, ROW])
        empty_rows = sb("empty_rows", [P, EMPTIES, ROW])

        tok_rows = sb("tok_rows", [P, 3, D])
        pos_rows = sb("pos_rows", [P, 2, D])
        nest_rows = sb("nest_rows", [TR, D])
        seg_rows = sb("seg_rows", [TR, D])
        bias_rows = sb("bias_rows", [TR, D])
        proj_diag = sb("proj_diag", [P, P])
        qkv_rows = sb("qkv_rows", [P, 3 * HC, D])
        out_rows = sb("out_rows", [P, HD])
        gate_w = sb("gate_w", [P, E])
        gate_b = sb("gate_b", [P, E])
        w1_all = sb("w1_all", [P, E, FF])
        w1_hi = sb("w1_hi", [P, E * FF], f32r)
        w1_lo = sb("w1_lo", [P, E * FF], f32r)
        w2_all = sb("w2_all", [P, FC, E, D])
        b1_all = sb("b1_all", [P, E * FF])
        b2_all = sb("b2_all", [P, E * D])
        rows_T = sb("rows_T", [P, 2 * P + 2 * TR])
        proj_T = sb("proj_T", [P, P])
        out_w = sb("out_w", [P, HC, D])
        pos_part = sb("pos_part", [P, 2, D])
        split_hi = sb("split_hi", [TR, 2, D], bf16)
        split_mid = sb("split_mid", [TR, 2, D], bf16)
        split_lo = sb("split_lo", [TR, 2, D], bf16)
        rest_one = sb("rest_one", [TR, 2, D])
        rest_two = sb("rest_two", [TR, 2, D])
        table = sb("table", [TR, 2, D], bf16)
        qkv_hi = sb("qkv_hi", [P, 3, HD], f32r)
        qkv_lo = sb("qkv_lo", [P, 3, HD], f32r)

        tokens = sb("tokens", [B, S], i32)
        zeros = sb("zeros", [B, S])
        delta = sb("delta", [B, S])
        other = sb("other", [B, S])
        depth = sb("depth", [B, S])
        floor = sb("floor", [B, S])
        nesting = sb("nesting", [B, S], bf16)
        seg_count = sb("seg_count", [B, S], i32)
        seg_int = sb("seg_int", [B, S], i32)
        segments = sb("segments", [B, S], bf16)
        row_of = sb("row_of", [TR, B * S], bf16)
        one_hot = sb("one_hot", [TR, 2, S], bf16)

        stats = sb("stats", [P, 2, 6])
        moments = sb("moments", [P, 2, 2, 2])
        rstd = sb("rstd", [P, 2, 2])
        shift = sb("shift", [P, 2, 2])
        xhat = sb("xhat", [P, 2, 2, D])
        xT_hi = sb("xT_hi", [P, 2, S], f32r)
        xT_lo = sb("xT_lo", [P, 2, S], f32r)

        qk_max = sb("qk_max", [P, 2, HEADS])
        q_prime = sb("q_prime", [P, 2, HD])
        k_prime = sb("k_prime", [P, 2, HD])
        v_ones = sb("v_ones", [P, 2, HEADS, DH + 1])
        context = sb("context", [P, 2, HC, 2, DH + 1])
        qT = sb("qT", [P, 2, HC, P])
        d_sum = sb("d_sum", [P, HEADS])
        d_inv = sb("d_inv", [P, HEADS])
        heads_out = sb("heads_out", [P, 2, HD])
        oT = sb("oT", [P, 2, HC, P])
        h = sb("h", [P, TILES, D])

        stats2 = sb("stats2", [P, 2, 6])
        moments2 = sb("moments2", [P, 2, 2, 2])
        rstd2 = sb("rstd2", [P, 2, 2])
        shift2 = sb("shift2", [P, 2, 2])
        rows = sb("rows", [P, 2, 2, ROW])
        x2T = sb("x2T", [P, 2, S])
        logits = sb("logits", [P, 2, E])
        top = sb("top", [P, 2, E])
        top_id = sb("top_id", [P, 2, E], u32)
        below = sb("below", [P, 2, E])
        exps = sb("exps", [P, 2, E])
        chosen = sb("chosen", [P, 2, TOP, E])
        chosen_w = sb("chosen_w", [P, 2, TOP, E])
        chosen_at = sb("chosen_at", [P, 2, TOP, E])
        mask = sb("mask", [P, 2, E], bf16)
        partial = sb("partial", [P, 2, E])
        denom = sb("denom", [P, 2])
        second_at = sb("second_at", [P, 2, E])
        weight = sb("weight", [P, 2, TOP])
        next_row = sb("next_row", [P, E])
        row_at = sb("row_at", [P, 2, E])
        row_id = sb("row_id", [P, 2, 2, TOP], i32)

        rows_used = sb("rows_used", [P, E])
        rows_up = sb("rows_up", [P, E], i32)
        tiles_of = sb("tiles_of", [P, E], i32)
        tiles_to = sb("tiles_to", [P, E])
        shift_at = sb("shift_at", [P, E + 1])
        shift_by = sb("shift_by", [P, E])
        past = qT[:, :, :, :].rearrange("p a c t -> p (a c t)")[:, 0:FTILES * E].rearrange("p (n e) -> p n e", e=E)
        past_by = oT[:, :, :, :].rearrange("p a c t -> p (a c t)")[:, 0:FTILES * E].rearrange("p (n e) -> p n e", e=E)
        expert_f = sb("expert_f", [P, FTILES])
        first_f = sb("first_f", [P, FTILES])
        tile_expert = sb("tile_expert", [P, FTILES + 2])
        digit = sb("digit", [P, RING])
        digits = sb("digits", [P, FTILES // RING, RING])
        group_f = sb("group_f", [P, FTILES // RING])
        group_experts = sb("group_experts", [P, FTILES // RING], i32)
        tile_row = sb("tile_row", [P, FTILES], i32)
        pad_at = sb("pad_at", [P, E], i32)

        spent = qkv_rows[:, :, :].rearrange("p a c -> p (a c)")
        slot_rows = spent[:, 0:RING * ROW].rearrange("p (a r) -> p a r", a=RING)
        y = heads_out[:, :, :].rearrange("p a c -> p (a c)")[:, 0:RING * D].rearrange("p (a d) -> p a d", a=RING)
        sT_hi = sb("sT_hi", [P, 2, P], f32r)
        sT_lo = sb("sT_lo", [P, 2, P], f32r)
        hidden = q_prime[:, :, :]
        hT = k_prime[:, :, :].rearrange("p a (c t) -> p a c t", c=FC)
        y_biased = spent[:, RING * ROW:RING * ROW + 2 * D].rearrange("p (a d) -> p a d", a=2)
        slot_w = sb("slot_w", [P, RING, 1])
        place = sb("place", [P, RING, 1], i32)

        Y_TILES = 8
        y_first = w1_all[:, :, :].rearrange("p e (t d) -> p (e t) d", d=D)
        y_second = b1_all[:, :].rearrange("p (t d) -> p t d", d=D)

        ps_q = pb("ps_q", [P, HD])
        ps_k = pb("ps_k", [P, HD])
        ps_vc = pb("ps_vc", [P, HD])
        ps_qT = pb("ps_qT", [P, HD])
        ps_out = pb("ps_out", [P, 2, HD])
        ps_oy = pb("ps_oy", [P, HD])
        ps_ln = pb("ps_ln", [P, HD])
        ps_ctx = ps_vc[:, 0:HC * (DH + 1)].rearrange("p (c d) -> p c d", c=HC)
        ps_slot, ps_up, ps_hT, ps_y = ps_ln, ps_q, ps_qT, (ps_oy, ps_vc)

        ids_dram = nc.dram_tensor("ids_dram", [2, B, S], bf16)
        slots_dram = nc.dram_tensor("slots_dram", [SLOTS, ROW], f32)
        y_dram = nc.dram_tensor("y_dram", [PLACES, D], f32)

        s_tok = sem("tokens_in")
        s_emb_w = sem("embedding_weights_in")
        s_att_w = sem("attention_weights_in")
        s_bias_w = sem("out_bias_in")
        s_gate_w = sem("gate_weights_in")
        s_w1 = sem("w1_in")
        s_ffn_w = sem("ffn_weights_in")
        s_zero = sem("rows_zeroed")
        s_ident = sem("ident_made")
        s_const = sem("constants_made")
        s_vec = sem("vector_chain")
        s_pool = sem("pool_chain")
        s_ids = sem("ids_made")
        s_ids_out = sem("ids_in_dram")
        s_row = sem("rows_in")
        s_t1 = sem("setup_transposed")
        s_t1c = sem("setup_copied")
        s_wT = sem("weight_products")
        s_wTc = sem("weight_products_split")
        s_hi = sem("weight_highs")
        s_ctx0 = sem("context_zeroed")

        s_hot = sem("one_hot_ready")
        s_emb = sem("embedding_done")
        s_h = sem("h_ready")
        s_mom, s_rstd = sem("moments_ready"), sem("rstd_ready")
        s_xhat = sem("xhat_ready")
        s_xT = sem("xT_done")
        s_xh, s_xl = sem("xT_hi_ready"), sem("xT_lo_ready")
        s_q, s_k, s_v = sem("q_done"), sem("k_done"), sem("v_done")
        s_qs, s_ks = sem("q_shifted"), sem("k_shifted")
        s_qp, s_kp, s_vo = sem("q_prime_ready"), sem("k_prime_ready"), sem("v_ready")
        s_c, s_cr = sem("context_done"), sem("context_ready")
        s_qT, s_qTr = sem("qT_done"), sem("qT_ready")
        s_o, s_or = sem("out_done"), sem("heads_out_ready")
        s_oT, s_oTr = sem("oT_done"), sem("oT_ready")
        s_y, s_h2 = sem("y_done"), sem("h2_ready")
        s_mom2, s_rstd2 = sem("moments2_ready"), sem("rstd2_ready")
        s_xhat2 = sem("xhat2_ready")
        s_x2T, s_x2Tr = sem("x2T_done"), sem("x2T_ready")
        s_lg, s_lgr = sem("logits_done"), sem("logits_read")
        s_below, s_exps = sem("logits_below_top"), sem("gate_exps_ready")
        s_mask = sem("mask_ready")
        s_rank, s_rankr = sem("ranks_done"), sem("ranks_read")
        s_id = sem("row_ids_ready")
        s_weighed = sem("weights_ready")
        s_slots = [sem(f"rows_in_slots{a}") for a in range(2)]
        s_w1h, s_w1l = sem("w1_hi_ready"), sem("w1_lo_ready")
        s_empty = sem("empty_rows_in_slots")
        s_tiles = sem("slot_tiles_known")
        s_groups = sem("group_experts_known")
        s_pad = sem("padding_in_slots")

        s_slot = [sem(f"slot_rows_in{a}") for a in range(RING)]
        s_sT, s_sh, s_sl = sem("slots_T_done"), sem("slots_T_hi_ready"), sem("slots_T_lo_ready")
        s_up, s_hid = sem("up_done"), sem("hidden_ready")
        s_hT, s_hTr = sem("hidden_T_done"), sem("hidden_T_ready")
        s_down, s_yb = sem("down_done"), sem("y_biased_ready")
        s_meta, s_yr = sem("slot_weights_ready"), sem("y_ready")
        s_placed = [sem(f"y_in_dram{a}") for a in range(RING)]
        s_back = [sem(f"y_in{c}") for c in range(TILES // Y_TILES)]
        s_tot = sem("total_ready")
        s_out = sem("out_written")

        block = ctx.enter_context(nc.Block())

        EMB_DMAS, ATT_DMAS, FFN_DMAS, GATE_DMAS = 8, 4, 3, 2

        @block.sync
        def _(sp):
            sp.dma_start(tokens[:, :], x[:, :]).then_inc(s_tok, 16)
            sp.dma_start(tok_rows[:, :, :], tok_w.rearrange("(a p) h -> p a h", p=P)).then_inc(s_emb_w, 16)
            sp.dma_start(pos_rows[:, :, :], pos_table[0:S, :].rearrange("(a p) h -> p a h", p=P)).then_inc(s_emb_w, 16)
            sp.wait_ge(s_zero, 1)
            for r in range(PARTS):
                sp.dma_start(nest_rows[SLOT * r:SLOT * r + NNEST, :], nest_table[:, :]).then_inc(s_emb_w, 16)
                sp.dma_start(seg_rows[SLOT * r + NNEST:SLOT * r + NNEST + NSEG, :], seg_table[:, :])\
                    .then_inc(s_emb_w, 16)
            for r in range(2):
                sp.dma_start(proj_diag[DH * r:DH * r + DH, DH * r:DH * r + DH], proj[:, :]).then_inc(s_att_w, 16)
            for r in range(PARTS):
                sp.dma_start(bias_rows[SLOT * r:SLOT * r + 1, :], b_out.rearrange("(o d) -> o d", o=1))\
                    .then_inc(s_bias_w, 16)
            sp.wait_ge(s_ids, 1)
            sp.dma_start(ids_dram[0, :, :], nesting[:, :]).then_inc(s_ids_out, 16)
            sp.wait_ge(s_ids, 2)
            sp.dma_start(ids_dram[1, :, :], segments[:, :]).then_inc(s_ids_out, 16)
            sp.wait_ge(s_ids_out, 32)
            for r in range(2 * PARTS):
                sp.dma_start(row_of[16 * r:16 * r + 16, :],
                             ids_dram[r % 2, :, :].rearrange("(o b) s -> o (b s)", o=1).to_broadcast([16, B * S]))\
                    .then_inc(s_row, 16)
            sp.dma_start(w1_all[:, :, :], w_one.rearrange("e d f -> d e f")).then_inc(s_w1, 16)
            sp.dma_start(b1_all[:, :], b_one.rearrange("(o e) f -> o (e f)", o=1).to_broadcast([P, E * FF]))\
                .then_inc(s_ffn_w, 16)
            sp.dma_start(b2_all[:, :], b_two.rearrange("(o e) d -> o (e d)", o=1).to_broadcast([P, E * D]))\
                .then_inc(s_ffn_w, 16)
            for e in range(E):
                sp.dma_start(w2_all[:, :, e, :], w_two[e, :, :].rearrange("(c p) d -> p c d", p=P)).then_inc(s_ffn_w, 16)
            sp.wait_ge(s_const, 1)
            sp.dma_start(slots_dram[EMPTY:SLOTS, :].rearrange("(n p) r -> p n r", p=P), empty_rows[:, :, :])\
                .then_inc(s_empty, 16)

            sp.wait_ge(s_tiles, 1)
            for e in range(E):
                at = sp.value_load(pad_at[0:1, e:e + 1], min_val=0, max_val=EMPTY - P)
                sp.dma_start(slots_dram[bass.ds(at, P), :], pad_rows[:, e, :]).then_inc(s_pad, 16)
            sp.wait_ge(s_pad, 16 * E)
            sp.wait_ge(s_empty, 16)
            for a in range(2):
                sp.wait_ge(s_slots[a], 16 * 2 * TOP * SEQS // 2)

            def load_slots(n, at):
                sp.dma_start(slot_rows[:, n % RING, :], slots_dram[bass.ds(at, P), :]).then_inc(s_slot[n % RING], 16)

            for n in range(AHEAD - 2):
                load_slots(n, sp.value_load(tile_row[0:1, n:n + 1], min_val=0, max_val=SLOTS - P))

            def load_ahead(n, a, i, before, after):
                if live(n + AHEAD, FTILES):
                    b = (a + AHEAD) % RING
                    wait(sp, s_yb, n + AHEAD - RING + 1)
                    at = sp.value_load(tile_row[0:1, span(n + AHEAD, 1)], min_val=0, max_val=SLOTS - P)
                    sp.dma_start(slot_rows[:, b, :], slots_dram[bass.ds(at, P), :]).then_inc(s_slot[b], 16)

            slot_tiles(sp, load_ahead)

            for a in range(RING):
                sp.wait_ge(s_placed[a], 16 * FTILES // RING)
            for c in range(TILES // Y_TILES):
                at = c * Y_TILES * P
                for k, dst in enumerate((y_first, y_second)):
                    sp.dma_start(dst[:, c * Y_TILES:c * Y_TILES + Y_TILES, :],
                                 y_dram[k * B * S + at:k * B * S + at + Y_TILES * P, :]
                                 .rearrange("(j p) d -> p j d", p=P)).then_inc(s_back[c], 16)

        @block.gpsimd
        def _(pool):
            step = Steps(pool, s_pool)
            nc.gpsimd.memset(nest_rows[:, :], 0.0)
            nc.gpsimd.memset(seg_rows[:, :], 0.0)
            nc.gpsimd.memset(bias_rows[:, :], 0.0)
            nc.gpsimd.memset(proj_diag[:, :], 0.0).then_inc(s_zero, 1)
            step.done(nc.gpsimd.memset(ident[:, :], 0.0))
            nc.gpsimd.affine_select(out=ident[:, :], in_=ident[:, :], compare_op=ALU.not_equal, fill=1.0, base=0,
                                    pattern=[[-1, P]], channel_multiplier=1).then_inc(s_ident, 1)
            nc.gpsimd.memset(minus_half[:, :], -0.5)
            nc.gpsimd.memset(ln_eps[:, :], LN_EPS)
            nc.gpsimd.memset(zero[:, :], 0.0)
            nc.gpsimd.memset(one[:, :], 1.0)
            nc.gpsimd.memset(minus_one[:, :], -1.0)
            nc.gpsimd.memset(top_eps[:, :], TOP_EPS)
            nc.gpsimd.memset(second[:, :], float(B * S))
            for r in range(PARTS):
                step.done(nc.gpsimd.iota(table_id[SLOT * r:SLOT * r + SLOT, :], [[0, 1]], base=0, channel_multiplier=1,
                                         allow_small_or_imprecise_dtypes=True))
            step.done(nc.gpsimd.memset(part_ones[:, :], 0.0))
            for r in range(PARTS):
                step.done(nc.gpsimd.memset(part_ones[SLOT * r:SLOT * r + 1, :], 1.0))
            nc.gpsimd.memset(context[:, :, :, :, :], 0.0).then_inc(s_ctx0, 1)
            for a in range(2):
                nc.gpsimd.memset(v_ones[:, a, :, DH:DH + 1], 1.0).then_inc(s_ctx0, 1)
            nc.gpsimd.memset(ones[:, :], 1.0)
            for r in range(RING):
                nc.gpsimd.memset(digit[:, r:r + 1], float(E ** (r + 1)))
            step.done(nc.gpsimd.memset(before[:, :], 1.0))
            nc.gpsimd.affine_select(out=before[:, :], in_=before[:, :], compare_op=ALU.is_gt, fill=0.0, base=0,
                                    pattern=[[1, P]], channel_multiplier=-1)
            nc.gpsimd.iota(expert_id[:, :], [[1, E]], base=0, channel_multiplier=0,
                           allow_small_or_imprecise_dtypes=True)
            nc.gpsimd.iota(expert_at[:, :], [[CAP, E + 1]], base=0, channel_multiplier=0,
                           allow_small_or_imprecise_dtypes=True)
            nc.gpsimd.iota(next_row[:, :], [[CAP, E]], base=0, channel_multiplier=0,
                           allow_small_or_imprecise_dtypes=True)
            nc.gpsimd.iota(token_id[:, :], [[P, TILES]], base=0, channel_multiplier=1,
                           allow_small_or_imprecise_dtypes=True)
            nc.gpsimd.iota(tile_id[:, :], [[1, FTILES]], base=0, channel_multiplier=0,
                           allow_small_or_imprecise_dtypes=True)
            step.add(nc.gpsimd.memset(pad_rows[:, :, :], 0.0))
            step.done(nc.gpsimd.memset(empty_rows[:, :, :], 0.0))
            nc.gpsimd.iota(pad_rows[:, :, D + E:ROW], [[P, E], [0, E]], base=CHOICES, channel_multiplier=1,
                           allow_small_or_imprecise_dtypes=True)
            nc.gpsimd.iota(empty_rows[:, :, D + E:ROW], [[P, EMPTIES], [0, E]], base=CHOICES + E * P,
                           channel_multiplier=1, allow_small_or_imprecise_dtypes=True).then_inc(s_const, 1)

            def take_wait():
                step.wait()
                step.add(nc.gpsimd.tensor_tensor(spare[:, :], minus_half[:, :], ln_eps[:, :], ALU.add))

            def scale_and_shift(p, a, mom, rs, sh, mom_sem, out_sem):
                pool.wait_ge(mom_sem, p + 1)
                step.done(nc.gpsimd.tensor_tensor(rs[:, a, :], mom[:, a, :, 1], ln_eps[:, :], ALU.add))
                step.done(nc.gpsimd.tensor_tensor(rs[:, a, :], rs[:, a, :], minus_half[:, :], ALU.pow))
                step.done(nc.gpsimd.tensor_tensor(sh[:, a, :], mom[:, a, :, 0], rs[:, a, :], ALU.mult))
                nc.gpsimd.tensor_tensor(sh[:, a, :], zero[:, :], sh[:, a, :], ALU.subtract).then_inc(out_sem, 1)

            def weigh(p, a):
                pool.wait_ge(s_exps, p + 1)
                terms, width = exps, E // 2
                while width:
                    step.done(nc.gpsimd.tensor_tensor(partial[:, :, 0:width], terms[:, :, 0:width],
                                                      terms[:, :, width:2 * width], ALU.add))
                    terms, width = partial, width // 2
                step.done(nc.gpsimd.tensor_tensor(denom[:, :], partial[:, :, 0], top_eps[:, :], ALU.mult))
                step.done(nc.gpsimd.tensor_tensor(denom[:, :], denom[:, :], exps[:, :, 1], ALU.add))
                step.done(nc.gpsimd.tensor_tensor(denom[:, :], denom[:, :], one[:, :], ALU.add))
                step.done(nc.gpsimd.tensor_tensor(weight[:, :, 0], denom[:, :], minus_one[:, :], ALU.pow))
                pool.wait_ge(s_mask, p + 1)
                step.add(nc.gpsimd.tensor_tensor(second_at[:, :, :], chosen[:, :, 1, :],
                                                 second[:, None, :].to_broadcast([P, 2, E]), ALU.mult))
                step.done(nc.gpsimd.tensor_tensor(weight[:, :, 1], weight[:, :, 0], exps[:, :, 1], ALU.mult))
                nc.gpsimd.tensor_tensor(rows[:, a, :, D + E:ROW], second_at[:, :, :],
                                        token_id[:, span(2 * p, 2), None].to_broadcast([P, 2, E]), ALU.add)
                step.done(nc.gpsimd.tensor_tensor(chosen_w[:, :, :, :], chosen[:, :, :, :],
                                                  weight[:, :, :, None].to_broadcast([P, 2, TOP, E]), ALU.mult))
                nc.gpsimd.tensor_tensor(rows[:, a, :, D:D + E], chosen_w[:, :, 0, :], chosen_w[:, :, 1, :],
                                        ALU.add).then_inc(s_weighed, 1)

            def scatter(p, a):
                pool.wait_ge(s_weighed, p + 1)
                pool.wait_ge(s_id, p + 1)
                take_wait()
                for j in range(2):
                    for k in range(TOP):
                        nc.gpsimd.indirect_dma_start(
                            slots_dram[:, :], bass.IndirectOffsetOnAxis(row_id[:, a, j, k:k + 1], 0),
                            rows[:, a, j, :], None).then_inc(s_slots[a], 16)

            def sequence(p, a, half):
                if live(p - 3):
                    weigh(p - 3, 1 - a)
                    scatter(p - 3, 1 - a)
                if live(p + 2):
                    scale_and_shift(p + 2, a, moments, rstd, shift, s_mom, s_rstd)
                if live(p - 1):
                    scale_and_shift(p - 1, 1 - a, moments2, rstd2, shift2, s_mom2, s_rstd2)
                if live(p):
                    pool.wait_ge(s_w1h, p + 1)
                    at = span(p * (E * FF // SEQS), E * FF // SEQS)
                    nc.gpsimd.tensor_tensor(w1_lo[:, at], w1_all[:, :, :].rearrange("p e f -> p (e f)")[:, at],
                                            w1_hi[:, at].bitcast(f32), ALU.subtract).then_inc(s_w1l, 1)

            sequences(pool, step, sequence, 34)

            def place_y(n, a, i, before, after):
                if live(n, FTILES):
                    pool.wait_ge(s_yr, n + 1)
                    take_wait()
                    nc.gpsimd.indirect_dma_start(
                        y_dram[:, :], bass.IndirectOffsetOnAxis(place[:, a, :], 0),
                        y[:, a, :], None).then_inc(s_placed[a], 16)

            slot_tiles(pool, place_y, step, RING)

        @block.scalar
        def _(act):
            act.dma_start(qkv_rows[:, :, :], w_qkv.rearrange("(a p) c -> p a c", p=P)).then_inc(s_att_w, 16)
            act.dma_start(out_rows[:, :], w_out[:, :]).then_inc(s_att_w, 16)
            act.dma_start(gate_w[:, :], w_gate[:, :]).then_inc(s_gate_w, 16)
            act.dma_start(gate_b[:, :], b_gate.rearrange("(o d) -> o d", o=1).to_broadcast([P, E])).then_inc(s_gate_w, 16)
            act.wait_ge(s_t1, 1)
            nc.scalar.activation(rows_T[:, :], ps_q[:, 0:2 * P + 2 * TR], ACT.Copy).then_inc(s_t1c, 1)
            act.wait_ge(s_t1, 2)
            nc.scalar.activation(proj_T[:, :], ps_k[:, 0:P], ACT.Copy).then_inc(s_t1c, 1)
            act.wait_ge(s_t1, 3)
            nc.scalar.activation(out_w[:, :, :], ps_qT[:, :], ACT.Copy).then_inc(s_hi, 1)
            act.wait_ge(s_t1, 4)
            nc.scalar.activation(qkv_hi[:, 2, :], ps_vc[:, :], ACT.Copy).then_inc(s_hi, 1)
            act.wait_ge(s_wT, 2)
            nc.scalar.activation(qkv_hi[:, 0, :], ps_out[:, 0, :], ACT.Copy, scale=DH ** -0.5).then_inc(s_hi, 1)
            act.wait_ge(s_wT, 3)
            nc.scalar.activation(qkv_hi[:, 1, :], ps_out[:, 1, :], ACT.Copy).then_inc(s_hi, 1)

            def xT_high(p, a):
                act.wait_ge(s_xT, p + 1)
                wait(act, s_v, 2 * p - 2)
                nc.scalar.activation(xT_hi[:, a, :], ps_ln[:, 0:S], ACT.Copy).then_inc(s_xh, 1)

            def q_exp(t, a):
                act.wait_ge(s_qs, t + 1)
                nc.scalar.activation(q_prime[:, a, :], q_prime[:, a, :], ACT.Exp).then_inc(s_qp, 1)

            def k_exp(t, a):
                act.wait_ge(s_ks, t + 1)
                nc.scalar.activation(k_prime[:, a, :], k_prime[:, a, :], ACT.Exp).then_inc(s_kp, 1)

            def v_copy(t, a):
                act.wait_ge(s_v, t + 1)
                wait(act, s_c, t - 1)
                nc.scalar.activation(v_ones[:, a, :, 0:DH], ps_vc[:, :].rearrange("p (h d) -> p h d", h=HEADS),
                                     ACT.Copy).then_inc(s_vo, 1)

            def qT_copy(t, a):
                act.wait_ge(s_qT, t + 1)
                wait(act, s_o, t - 1)
                nc.scalar.activation(qT[:, a, :, :], ps_qT[:, :], ACT.Copy).then_inc(s_qTr, 1)

            def context_copy(t, a):
                act.wait_ge(s_c, t + 1)
                nc.scalar.activation(context[0:DH, a, :, 0, :], ps_ctx[0:DH], ACT.Copy)
                nc.scalar.activation(context[DH:P, a, :, 1, :], ps_ctx[DH:P], ACT.Copy).then_inc(s_cr, 1)

            def oT_copy(t, a):
                act.wait_ge(s_oT, t + 1)
                nc.scalar.activation(oT[:, a, :, :], ps_oy[:, :], ACT.Copy).then_inc(s_oTr, 1)

            def x2T_copy(p, a):
                act.wait_ge(s_x2T, p + 1)
                nc.scalar.activation(x2T[:, a, :], ps_ln[:, 0:S], ACT.Copy).then_inc(s_x2Tr, 1)

            def w1_high(p):
                at = span(p * (E * FF // SEQS), E * FF // SEQS)
                nc.scalar.activation(w1_hi[:, at], w1_all[:, :, :].rearrange("p e f -> p (e f)")[:, at],
                                     ACT.Copy).then_inc(s_w1h, 1)

            def normalize(p, a, rs, sh, dst, rstd_sem, out_sem):
                act.wait_ge(rstd_sem, p + 1)
                for k in range(2):
                    last = nc.scalar.activation(dst(k), h[:, span(2 * p + k, 1), :].rearrange("p o d -> p (o d)"),
                                                ACT.Identity, bias=sh[:, a, k:k + 1], scale=rs[:, a, k:k + 1])
                last.then_inc(out_sem, 1)

            def sequence(p, a, half):
                for j in range(2):
                    t = 2 * p + j
                    if j == 1 and live(p - 2):
                        x2T_copy(p - 2, a)
                    if live(p):
                        context_copy(t, j)
                    if live(t - 1, TILES):
                        oT_copy(t - 1, 1 - j)
                    if live(t + 1, TILES):
                        q_exp(t + 1, 1 - j)
                    if j == 0 and live(p + 1):
                        xT_high(p + 1, 1 - a)
                    if live(t + 1, TILES):
                        k_exp(t + 1, 1 - j)
                    if j == 0 and live(p - 2):
                        wait(act, s_slots[a], 16 * 2 * TOP * (half - 1))
                        normalize(p - 2, a, rstd2, shift2, lambda k: rows[:, a, k, 0:D], s_rstd2, s_xhat2)
                    if live(t + 1, TILES):
                        v_copy(t + 1, 1 - j)
                    if live(t + 1, TILES):
                        qT_copy(t + 1, 1 - j)
                    if j == 1 and live(p - 2):
                        act.wait_ge(s_below, p - 1)
                        wait(act, s_weighed, p - 2)
                        nc.scalar.activation(exps[:, :, :], below[:, :, :], ACT.Exp).then_inc(s_exps, 1)
                    if j == 1 and live(p + 2):
                        wait(act, s_xT, p + 1)
                        normalize(p + 2, a, rstd, shift, lambda k: xhat[:, a, k, :], s_rstd, s_xhat)
                    if j == 1 and live(p):
                        w1_high(p)

            act.wait_ge(s_ctx0, 3)
            act.wait_ge(s_w1, 16)
            sequences(act, None, sequence)

            def slot_tile(n, a, i, before, after):
                if live(n, FTILES):
                    act.wait_ge(s_hT, n + 1)
                    wait(act, s_down, n - 1)
                    nc.scalar.activation(hT[:, a % 2, :, :], ps_hT[:, :], ACT.Relu).then_inc(s_hTr, 1)
                if live(n + 2, FTILES):
                    act.wait_ge(s_sT, n + 3)
                    wait(act, s_up, n + 1)
                    nc.scalar.activation(sT_hi[:, a % 2, :], ps_slot[:, 0:P], ACT.Copy).then_inc(s_sh, 1)
                if live(n - 2, FTILES):
                    b = (a - 2) % RING
                    act.wait_ge(s_yb, n - 1)
                    if live(n - 2 - RING, FTILES):
                        act.wait_ge(s_placed[b], 16 * (i if b == a - 2 else i - 1))
                    nc.scalar.activation(y[:, b, :], y_biased[:, b % 2, :], ACT.Copy,
                                         scale=slot_w[:, b, :]).then_inc(s_yr, 1)

            slot_tiles(act, slot_tile)

            for c in range(TILES // Y_TILES):
                act.wait_ge(s_tot, c + 1)
                act.dma_start(out.rearrange("b s d -> (b s) d")[c * Y_TILES * P:(c + 1) * Y_TILES * P, :]
                              .rearrange("(j p) d -> p j d", p=P),
                              y_first[:, c * Y_TILES:c * Y_TILES + Y_TILES, :]).then_inc(s_out, 16)
            act.wait_ge(s_out, 16 * TILES // Y_TILES)

        @block.vector
        def _(dve):
            step = Steps(dve, s_vec)
            step.done(nc.vector.memset(zeros[:, :], 0.0))
            dve.wait_ge(s_tok, 16)
            step.done(nc.vector.tensor_scalar(delta[:, :], tokens[:, :], 40, None, ALU.is_equal))
            for code in (123, 91):
                step.done(nc.vector.scalar_tensor_tensor(delta[:, :], tokens[:, :], code, delta[:, :],
                                                         ALU.is_equal, ALU.add))
            step.done(nc.vector.tensor_scalar(other[:, :], tokens[:, :], 41, None, ALU.is_equal))
            for code in (125, 93):
                step.done(nc.vector.scalar_tensor_tensor(other[:, :], tokens[:, :], code, other[:, :],
                                                         ALU.is_equal, ALU.add))
            step.done(nc.vector.tensor_tensor(delta[:, :], delta[:, :], other[:, :], ALU.subtract))
            step.done(nc.vector.tensor_tensor_scan(depth[:, :], delta[:, :], zeros[:, :], 0.0, ALU.add, ALU.add))
            step.done(nc.vector.tensor_tensor_scan(floor[:, :], depth[:, :], zeros[:, :], 0.0, ALU.min, ALU.min))
            step.done(nc.vector.tensor_tensor(depth[:, :], depth[:, :], floor[:, :], ALU.subtract))
            nc.vector.tensor_scalar(nesting[:, :], depth[:, :], float(NNEST - 1), 0.0, ALU.min, ALU.max)\
                .then_inc(s_ids, 1)
            step.done(nc.vector.tensor_scalar(other[:, :], tokens[:, :], 39990, None, ALU.is_gt))
            step.done(nc.vector.tensor_tensor_scan(seg_count[:, :], other[:, :], zeros[:, :], 0.0, ALU.add, ALU.add))
            step.done(nc.vector.tensor_scalar(seg_int[:, :], seg_count[:, :], NSEG - 1, None, ALU.bitwise_and))
            nc.vector.tensor_scalar(segments[:, :], seg_int[:, :], float(NNEST), None, ALU.add).then_inc(s_ids, 1)

            dve.wait_ge(s_wT, 1)
            step.done(nc.vector.tensor_copy(pos_part[:, :, :], ps_oy[:, 0:2 * D].rearrange("p (a d) -> p a d", a=2)))
            dve.wait_ge(s_bias_w, 16 * PARTS)
            step.add(nc.vector.tensor_copy(rest_two[:, 0, :], ps_oy[0:TR, 2 * D:3 * D]))
            step.done(nc.vector.tensor_copy(rest_two[:, 1, :], bias_rows[:, :]))
            step.done(nc.vector.tensor_copy(split_hi[:, :, :], rest_two[:, :, :]))
            step.done(nc.vector.tensor_tensor(rest_one[:, :, :], rest_two[:, :, :], split_hi[:, :, :], ALU.subtract))
            step.done(nc.vector.tensor_copy(split_mid[:, :, :], rest_one[:, :, :]))
            step.done(nc.vector.tensor_tensor(rest_two[:, :, :], rest_one[:, :, :], split_mid[:, :, :], ALU.subtract))
            step.done(nc.vector.tensor_copy(split_lo[:, :, :], rest_two[:, :, :]))
            for r, part in enumerate((split_hi, split_mid, split_lo)):
                last = nc.vector.tensor_copy(table[SLOT * r:SLOT * r + SLOT, :, :], part[SLOT * r:SLOT * r + SLOT, :, :])
            last.then_inc(s_wTc, 1)
            dve.wait_ge(s_hi, 2)
            nc.vector.tensor_tensor(qkv_lo[:, 2, :], ps_vc[:, :], qkv_hi[:, 2, :].bitcast(f32), ALU.subtract)
            dve.wait_ge(s_hi, 3)
            nc.vector.scalar_tensor_tensor(qkv_lo[:, 0, :], ps_out[:, 0, :], DH ** -0.5, qkv_hi[:, 0, :].bitcast(f32),
                                           ALU.mult, ALU.subtract)
            dve.wait_ge(s_hi, 4)
            nc.vector.tensor_tensor(qkv_lo[:, 1, :], ps_out[:, 1, :], qkv_hi[:, 1, :].bitcast(f32),
                                    ALU.subtract).then_inc(s_wTc, 1)

            def hot(p, a):
                wait(dve, s_emb, p - 1)
                nc.vector.tensor_scalar(one_hot[:, a, :], row_of[:, span(p * S, S)], table_id[:, 0:1], None,
                                        ALU.is_equal).then_inc(s_hot, 1)

            def stats_of(p, st):
                for j in range(2):
                    last = nc.vector.bn_stats(st[:, j, :], h[:, span(2 * p + j, 1), :].rearrange("p o d -> p (o d)"))
                step.add(last)

            def moments_of(a, st, mom, out_sem):
                for j in range(2):
                    last = nc.vector.bn_aggr(mom[:, a, j, :], st[:, j, :])
                last.then_inc(out_sem, 1)

            def embed(p, a):
                dve.wait_ge(s_emb, p + 1)
                nc.vector.tensor_tensor(h[:, span(2 * p, 2), :], ps_ln[:, 0:S].rearrange("p (a d) -> p a d", a=2),
                                        pos_part[:, :, :], ALU.add).then_inc(s_h, 1)

            def xT_low(p, a):
                dve.wait_ge(s_xh, p + 1)
                nc.vector.tensor_tensor(xT_lo[:, a, :], ps_ln[:, 0:S], xT_hi[:, a, :].bitcast(f32),
                                        ALU.subtract).then_inc(s_xl, 1)

            def head_max(t, ps, n, done_sem):
                dve.wait_ge(done_sem, t + 1)
                step.add(nc.vector.tensor_reduce(qk_max[:, n, :], ps[:, :].rearrange("p (h f) -> p h f", h=HEADS),
                                                 AX.X, ALU.max))

            def subtract_max(t, a, ps, dst, n, free_sem, out_sem):
                wait(dve, free_sem, t - 1)
                nc.vector.tensor_tensor(dst[:, a, :].rearrange("p (h f) -> p h f", h=HEADS),
                                        ps[:, :].rearrange("p (h f) -> p h f", h=HEADS),
                                        qk_max[:, n, :, None].to_broadcast([P, HEADS, DH]),
                                        ALU.subtract).then_inc(out_sem, 1)

            heads = ps_out[:, :, 0:HC * (DH + 1)].rearrange("p r (c d) -> p r c d", c=HC)

            def divisor(t):
                dve.wait_ge(s_o, t + 1)
                step.add(nc.vector.tensor_scalar(d_sum[:, :].rearrange("p (r c) -> p r c", r=2), heads[:, :, :, DH],
                                                 D_EPS, None, ALU.add))

            def invert():
                step.add(nc.vector.reciprocal(d_inv[:, :], d_sum[:, :]))

            def divide(t, a):
                nc.vector.tensor_tensor(
                    heads_out[:, a, :].rearrange("p (r c d) -> p r c d", r=2, c=HC), heads[:, :, :, 0:DH],
                    d_inv[:, :].rearrange("p (r c) -> p r c", r=2)[:, :, :, None].to_broadcast([P, 2, HC, DH]),
                    ALU.mult).then_inc(s_or, 1)

            def residual(t):
                dve.wait_ge(s_y, t + 1)
                at = h[:, span(t, 1), :].rearrange("p o d -> p (o d)")
                nc.vector.tensor_tensor(at, ps_oy[:, 0:D], at, ALU.add).then_inc(s_h2, 1)

            def read_logits(p):
                dve.wait_ge(s_lg, p + 1)
                nc.vector.tensor_tensor(logits[:, :, :], ps_ln[:, 0:2 * E].rearrange("p (j e) -> p j e", j=2),
                                        gate_b[:, None, :].to_broadcast([P, 2, E]), ALU.add).then_inc(s_lgr, 1)

            def find_top():
                for j in range(2):
                    last = nc.vector.max(top[:, j, :], logits[:, j, :])
                step.add(last)

            def find_top_ids():
                for j in range(2):
                    last = nc.vector.max_index(top_id[:, j, :], top[:, j, :], logits[:, j, :])
                step.add(last)

            def below_top():
                nc.vector.tensor_tensor(below[:, :, :], top[:, :, :], top[:, :, 0:1].to_broadcast([P, 2, E]),
                                        ALU.subtract).then_inc(s_below, 1)

            def choose(p):
                wait(dve, s_weighed, p)
                step.done(nc.vector.tensor_tensor(
                    chosen[:, :, :, :], expert_id[:, None, None, :].to_broadcast([P, 2, TOP, E]),
                    top_id[:, :, 0:TOP, None].to_broadcast([P, 2, TOP, E]), ALU.is_equal))
                nc.vector.tensor_tensor(mask[:, :, :], chosen[:, :, 0, :], chosen[:, :, 1, :], ALU.add)\
                    .then_inc(s_mask, 1)

            def read_ranks(p):
                dve.wait_ge(s_rank, p + 1)
                step.add(nc.vector.tensor_tensor(row_at[:, :, :], ps_ln[:, 0:2 * E].rearrange("p (j e) -> p j e", j=2),
                                                 next_row[:, None, :].to_broadcast([P, 2, E]), ALU.add))

            def move_next_row():
                nc.vector.tensor_tensor(next_row[:, :], ps_ln[:, 2 * E:3 * E], next_row[:, :], ALU.add)\
                    .then_inc(s_rankr, 1)

            def rows_of_choices():
                step.add(nc.vector.tensor_tensor(chosen_at[:, :, :, :], chosen[:, :, :, :],
                                                 row_at[:, :, None, :].to_broadcast([P, 2, TOP, E]), ALU.mult))

            def give_rows(a):
                nc.vector.tensor_reduce(row_id[:, a, :, :], chosen_at[:, :, :, :], AX.X, ALU.max).then_inc(s_id, 1)

            def even(p, a):
                t = 2 * p
                more = live(t + 1, TILES)
                ranks = live(p - 3)
                if live(t - 2, TILES):
                    residual(t - 2)
                if more:
                    head_max(t + 1, ps_q, 0, s_q)
                if ranks:
                    read_ranks(p - 3)
                if more or ranks:
                    step.wait()
                if more:
                    subtract_max(t + 1, 1, ps_q, q_prime, 0, s_qT, s_qs)
                if ranks:
                    move_next_row()
                    rows_of_choices()
                if more:
                    head_max(t + 1, ps_k, 1, s_k)
                if more or ranks:
                    step.wait()
                if more:
                    subtract_max(t + 1, 1, ps_k, k_prime, 1, s_c, s_ks)
                if ranks:
                    give_rows(1 - a)
                if live(p):
                    divisor(t)
                if live(p + 1):
                    xT_low(p + 1, 1 - a)
                if live(p):
                    step.wait()
                    invert()
                if live(p + 2):
                    hot(p + 2, a)
                if live(p):
                    step.wait()
                    divide(t, 0)

            def odd(p, a):
                t = 2 * p + 1
                more = live(t + 1, TILES)
                if live(t - 2, TILES):
                    residual(t - 2)
                if more:
                    head_max(t + 1, ps_q, 0, s_q)
                if live(p + 2):
                    embed(p + 2, a)
                if more:
                    step.wait()
                if live(p - 1):
                    dve.wait_ge(s_h2, 2 * p)
                if live(p + 2):
                    dve.wait_ge(s_h, p + 3)
                if more:
                    subtract_max(t + 1, 0, ps_q, q_prime, 0, s_qT, s_qs)
                    head_max(t + 1, ps_k, 1, s_k)
                if live(p + 2):
                    stats_of(p + 2, stats)
                if live(p - 1):
                    stats_of(p - 1, stats2)
                if live(p - 2):
                    read_logits(p - 2)
                step.wait()
                if live(p - 2):
                    dve.wait_ge(s_lgr, p - 1)
                if more:
                    subtract_max(t + 1, 0, ps_k, k_prime, 1, s_c, s_ks)
                if live(p + 2):
                    moments_of(a, stats, moments, s_mom)
                if live(p - 1):
                    moments_of(1 - a, stats2, moments2, s_mom2)
                if live(p - 2):
                    find_top()
                if live(p):
                    divisor(t)
                if live(p) or live(p - 2):
                    step.wait()
                if live(p):
                    invert()
                if live(p - 2):
                    find_top_ids()
                    below_top()
                if live(p) or live(p - 2):
                    step.wait()
                if live(p):
                    divide(t, 1)
                if live(p - 2):
                    choose(p - 2)

            def sequence(p, a, half):
                even(p, a)
                odd(p, a)

            dve.wait_ge(s_row, 16 * 2 * PARTS)
            dve.wait_ge(s_gate_w, 16 * GATE_DMAS)
            dve.wait_ge(s_const, 1)
            sequences(dve, step, sequence, 30)

            step.done(nc.vector.tensor_tensor(rows_used[:, :], next_row[:, :], expert_at[:, 0:E], ALU.subtract))
            step.done(nc.vector.tensor_scalar(rows_up[:, :], rows_used[:, :], float(P - 1), None, ALU.add))
            step.done(nc.vector.tensor_scalar(tiles_of[:, :], rows_up[:, :], P.bit_length() - 1, None,
                                              ALU.logical_shift_right))
            step.add(nc.vector.memset(tile_expert[:, :], 0.0))
            step.done(nc.vector.memset(shift_at[:, :], 0.0))
            step.done(nc.vector.tensor_tensor_scan(tiles_to[:, :], tiles_of[:, :], shift_at[:, 0:E], 0.0, ALU.add, ALU.add))
            step.done(nc.vector.scalar_tensor_tensor(shift_at[:, 1:E + 1], tiles_to[:, :], -float(P), expert_at[:, 1:E + 1],
                                                     ALU.mult, ALU.add))
            step.done(nc.vector.tensor_tensor(shift_by[:, :], shift_at[:, 1:E + 1], shift_at[:, 0:E], ALU.subtract))
            step.done(nc.vector.tensor_tensor(past[:, :, :], tiles_to[:, None, :].to_broadcast([P, FTILES, E]),
                                              tile_id[:, :, None].to_broadcast([P, FTILES, E]), ALU.is_le))
            step.add(nc.vector.tensor_reduce(expert_f[:, :], past[:, :, :], AX.X, ALU.add))
            step.done(nc.vector.tensor_tensor(past_by[:, :, :], past[:, :, :],
                                              shift_by[:, None, :].to_broadcast([P, FTILES, E]), ALU.mult))
            step.done(nc.vector.tensor_reduce(first_f[:, :], past_by[:, :, :], AX.X, ALU.add))
            nc.vector.scalar_tensor_tensor(tile_row[:, :], tile_id[:, :], float(P), first_f[:, :], ALU.mult, ALU.add)
            nc.vector.tensor_scalar(tile_expert[:, 1:FTILES + 1], expert_f[:, :], float(E - 1), None, ALU.min)
            nc.vector.tensor_copy(pad_at[:, :], next_row[:, :]).then_inc(s_tiles, 1)
            dve.wait_ge(s_tiles, 1)
            group = tile_expert[:, 1:FTILES + 1].rearrange("p (g r) -> p g r", r=RING)
            after = tile_expert[:, 2:FTILES + 2].rearrange("p (g r) -> p g r", r=RING)[:, :, RING - 1]
            previous = tile_expert[:, 0:FTILES].rearrange("p (g r) -> p g r", r=RING)[:, :, 0]
            step.done(nc.vector.tensor_tensor(digits[:, :, :], group,
                                              digit[:, None, :].to_broadcast([P, FTILES // RING, RING]), ALU.mult))
            step.done(nc.vector.tensor_reduce(group_f[:, :], digits[:, :, :], AX.X, ALU.add))
            step.done(nc.vector.scalar_tensor_tensor(group_f[:, :], after, float(E ** (RING + 1)), group_f[:, :],
                                                     ALU.mult, ALU.add))
            nc.vector.tensor_tensor(group_experts[:, :], previous, group_f[:, :], ALU.add).then_inc(s_groups, 1)
            dve.wait_ge(s_groups, 1)
            dve.wait_ge(s_ffn_w, 16 * (E + 2))

            def slot_tile(n, a, i, before, after):
                if live(n + 1, FTILES):
                    bias = dve.snap(after * FF)
                    dve.wait_ge(s_up, n + 2)
                    wait(dve, s_hT, n)
                    nc.vector.tensor_tensor(hidden[:, (a + 1) % 2, :], ps_up[:, :], b1_all[:, bass.ds(bias, FF)],
                                            ALU.add).then_inc(s_hid, 1)
                if live(n + 2, FTILES):
                    dve.wait_ge(s_sh, n + 3)
                    nc.vector.tensor_tensor(sT_lo[:, a % 2, :], ps_slot[:, 0:P], sT_hi[:, a % 2, :].bitcast(f32),
                                            ALU.subtract).then_inc(s_sl, 1)
                if live(n - 1, FTILES):
                    b = (a - 1) % RING
                    weight_at, place_at = dve.snap(before + D), dve.snap(before + (D + E))
                    bias = dve.snap(before * D)
                    if live(n - 1 - RING, FTILES):
                        dve.wait_ge(s_placed[b], 16 * (i if b == a - 1 else i - 1))
                    nc.vector.tensor_copy(slot_w[:, b, :], slot_rows[:, b, bass.ds(weight_at, 1)])
                    nc.vector.tensor_copy(place[:, b, :], slot_rows[:, b, bass.ds(place_at, 1)])
                    dve.wait_ge(s_down, n)
                    wait(dve, s_yr, n - 2)
                    nc.vector.tensor_tensor(y_biased[:, b % 2, :], ps_y[b % 2][:, 0:D], b2_all[:, bass.ds(bias, D)],
                                            ALU.add).then_inc(s_yb, 1)

            slot_tiles(dve, slot_tile, groups=group_experts)

            for c in range(TILES // Y_TILES):
                at = slice(c * Y_TILES, c * Y_TILES + Y_TILES)
                dve.wait_ge(s_back[c], 16 * TOP)
                step.done(nc.vector.tensor_tensor(y_first[:, at, :], y_first[:, at, :], y_second[:, at, :], ALU.add))
                nc.vector.tensor_tensor(y_first[:, at, :], y_first[:, at, :], h[:, at, :], ALU.add).then_inc(s_tot, 1)

        @block.tensor
        def _(pe):
            pe.wait_ge(s_ident, 1)
            pe.wait_ge(s_emb_w, 16 * EMB_DMAS)
            idn = ident[:, :]
            for a in range(2):
                nc.tensor.transpose(ps_q[:, a * P:a * P + P], pos_rows[:, a, :], idn)
            nc.tensor.transpose(ps_q[:, 2 * P:2 * P + TR], nest_rows[:, :], ident[0:TR, 0:TR])
            nc.tensor.transpose(ps_q[:, 2 * P + TR:2 * P + 2 * TR], seg_rows[:, :], ident[0:TR, 0:TR]).then_inc(s_t1, 1)
            pe.wait_ge(s_att_w, 16 * ATT_DMAS)
            nc.tensor.transpose(ps_k[:, 0:P], proj_diag[:, :], idn).then_inc(s_t1, 1)
            for c in range(HC):
                last = nc.tensor.transpose(ps_qT[:, c * P:c * P + P], out_rows[:, c * P:c * P + P], idn)
            last.then_inc(s_t1, 1)
            for c in range(HC):
                last = nc.tensor.transpose(ps_vc[:, c * P:c * P + P], qkv_rows[:, 2 * HC + c, :], idn)
            last.then_inc(s_t1, 1)
            pe.wait_ge(s_t1c, 1)
            for a in range(2):
                nc.tensor.matmul(ps_oy[:, a * D:a * D + D], rows_T[:, a * P:a * P + P], tok_rows[:, 0, :],
                                 start=True, stop=True)
            nc.tensor.matmul(ps_oy[0:TR, 2 * D:3 * D], rows_T[:, 2 * P:2 * P + TR], tok_rows[:, 1, :],
                             start=True, stop=False)
            nc.tensor.matmul(ps_oy[0:TR, 2 * D:3 * D], rows_T[:, 2 * P + TR:2 * P + 2 * TR], tok_rows[:, 2, :],
                             start=False, stop=True).then_inc(s_wT, 1)
            pe.wait_ge(s_t1c, 2)
            for n in range(2):
                for c in range(HC):
                    last = nc.tensor.matmul(ps_out[:, n, c * P:c * P + P], qkv_rows[:, n * HC + c, :], proj_T[:, :],
                                            start=True, stop=True)
                last.then_inc(s_wT, 1)
            pe.wait_ge(s_wTc, 2)
            pe.wait_ge(s_hi, 4)
            pe.wait_ge(s_const, 1)
            pe.wait_ge(s_gate_w, 16 * GATE_DMAS)

            def embed(p, a):
                pe.wait_ge(s_hot, p + 1)
                wait(pe, s_x2Tr, p - 3)
                for j in range(2):
                    last = nc.tensor.matmul(ps_ln[:, j * D:j * D + D], one_hot[:, a, j * P:j * P + P], table[:, 0, :],
                                            start=True, stop=True)
                last.then_inc(s_emb, 1)

            def x_transpose(p, a):
                pe.wait_ge(s_xhat, p + 1)
                if live(p - 4):
                    pe.wait_ge(s_rankr, p - 3)
                else:
                    pe.wait_ge(s_h, p + 1)
                for j in range(2):
                    last = nc.tensor.transpose(ps_ln[:, j * P:j * P + P], xhat[:, a, j, :], idn)
                last.then_inc(s_xT, 1)

            def product(n, ps, a, j, out_sem):
                for m, (w, xt) in enumerate(((qkv_hi, xT_hi), (qkv_lo, xT_hi), (qkv_hi, xT_lo))):
                    last = nc.tensor.matmul(ps[:, :], xt[:, a, j * P:j * P + P], w[:, n, :], start=(m == 0), stop=(m == 2))
                last.then_inc(out_sem, 1)

            def q_product(t, p, a, j):
                pe.wait_ge(s_xl, p + 1)
                wait(pe, s_qs, t)
                product(0, ps_q, a, j, s_q)

            def k_product(t, a, j):
                wait(pe, s_ks, t)
                product(1, ps_k, a, j, s_k)

            def v_product(t, a, j):
                wait(pe, s_cr, t)
                product(2, ps_vc, a, j, s_v)

            def q_transpose(t, a):
                pe.wait_ge(s_qp, t + 1)
                wait(pe, s_qTr, t)
                for c in range(HC):
                    last = nc.tensor.transpose(ps_qT[:, c * P:c * P + P], q_prime[:, a, c * P:c * P + P], idn)
                last.then_inc(s_qT, 1)

            def context_product(t, a):
                pe.wait_ge(s_kp, t + 1)
                pe.wait_ge(s_vo, t + 1)
                for n in range(HEADS):
                    r = DH * (n % 2)
                    last = nc.tensor.matmul(ps_ctx[r:r + DH, n // 2, :], k_prime[:, a, n * DH:n * DH + DH],
                                            v_ones[:, a, n, :], start=True, stop=True)
                last.then_inc(s_c, 1)

            def out_product(t, a):
                pe.wait_ge(s_cr, t + 1)
                pe.wait_ge(s_qTr, t + 1)
                wait(pe, s_or, t)
                for c in range(HC):
                    at = c % 2 * 2 * (DH + 1)
                    last = nc.tensor.matmul(ps_out[:, c // 2, at:at + 2 * (DH + 1)], qT[:, a, c, :],
                                            context[:, a, c, :, :].rearrange("p r d -> p (r d)"), start=True, stop=True)
                last.then_inc(s_o, 1)

            def o_transpose(t, a):
                pe.wait_ge(s_or, t + 1)
                wait(pe, s_h2, t)
                for c in range(HC):
                    last = nc.tensor.transpose(ps_oy[:, c * P:c * P + P], heads_out[:, a, c * P:c * P + P], idn)
                last.then_inc(s_oT, 1)

            def y_product(t, a):
                pe.wait_ge(s_oTr, t + 1)
                nc.tensor.matmul(ps_oy[:, 0:D], part_ones[:, :], table[:, 1, :], start=True, stop=False)
                for c in range(HC):
                    last = nc.tensor.matmul(ps_oy[:, 0:D], oT[:, a, c, :], out_w[:, c, :], start=False, stop=(c == HC - 1))
                last.then_inc(s_y, 1)

            def x2_transpose(p, a):
                pe.wait_ge(s_xhat2, p + 1)
                if live(p + 3):
                    pe.wait_ge(s_xl, p + 4)
                else:
                    pe.wait_ge(s_rankr, p)
                for j in range(2):
                    last = nc.tensor.transpose(ps_ln[:, j * P:j * P + P], rows[:, a, j, 0:D], idn)
                last.then_inc(s_x2T, 1)

            def gate_product(p, a):
                pe.wait_ge(s_x2Tr, p + 1)
                if live(p + 4):
                    pe.wait_ge(s_h, p + 5)
                for j in range(2):
                    last = nc.tensor.matmul(ps_ln[:, j * E:j * E + E], x2T[:, a, j * P:j * P + P], gate_w[:, :],
                                            start=True, stop=True)
                last.then_inc(s_lg, 1)

            def rank_product(p):
                pe.wait_ge(s_mask, p + 1)
                nc.tensor.matmul(ps_ln[:, 0:E], before[:, :], mask[:, 0, :], start=True, stop=True)
                nc.tensor.matmul(ps_ln[:, E:2 * E], before[:, :], mask[:, 1, :], start=True, stop=False)
                nc.tensor.matmul(ps_ln[:, E:2 * E], ones[:, :], mask[:, 0, :], start=False, stop=True)
                nc.tensor.matmul(ps_ln[:, 2 * E:3 * E], ones[:, :], mask[:, 0, :], start=True, stop=False)
                nc.tensor.matmul(ps_ln[:, 2 * E:3 * E], ones[:, :], mask[:, 1, :], start=False, stop=True)\
                    .then_inc(s_rank, 1)

            def sequence(p, a, half):
                for j in range(2):
                    t = 2 * p + j
                    np_, na, nj = (p, a, 1) if j == 0 else (p + 1, 1 - a, 0)
                    more = live(t + 1, TILES)
                    if more:
                        q_product(t + 1, np_, na, nj)
                    if j == 1 and live(p + 2):
                        embed(p + 2, a)
                    if live(p):
                        context_product(t, j)
                    if j == 0 and live(p - 3):
                        rank_product(p - 3)
                    if live(t - 1, TILES):
                        o_transpose(t - 1, 1 - j)
                    if more:
                        k_product(t + 1, na, nj)
                    if j == 1 and live(p - 2):
                        gate_product(p - 2, a)
                    if live(p):
                        out_product(t, j)
                    if j == 0 and live(p + 1):
                        x_transpose(p + 1, 1 - a)
                    if more:
                        v_product(t + 1, na, nj)
                        q_transpose(t + 1, 1 - j)
                    if live(t - 1, TILES):
                        y_product(t - 1, 1 - j)
                    if j == 0 and live(p - 2):
                        x2_transpose(p - 2, a)

            sequences(pe, None, sequence)

            pe.wait_ge(s_groups, 1)
            pe.wait_ge(s_w1l, SEQS)
            pe.wait_ge(s_ffn_w, 16 * (E + 2))

            def slot_tile(n, a, i, before, after):
                if live(n, FTILES):
                    pe.wait_ge(s_hid, n + 1)
                    wait(pe, s_hTr, n)
                    for c in range(FC):
                        last = nc.tensor.transpose(ps_hT[:, c * P:c * P + P], hidden[:, a % 2, c * P:c * P + P], idn)
                    last.then_inc(s_hT, 1)
                if live(n + 1, FTILES):
                    at = pe.snap(after * FF)
                    pe.wait_ge(s_sl, n + 2)
                    wait(pe, s_hid, n + 1)
                    for m, (w, st) in enumerate(((w1_hi, sT_hi), (w1_lo, sT_hi), (w1_hi, sT_lo))):
                        last = nc.tensor.matmul(ps_up[:, :], st[:, (a + 1) % 2, :], w[:, bass.ds(at, FF)],
                                                start=(m == 0), stop=(m == 2))
                    last.then_inc(s_up, 1)
                if live(n + 2, FTILES):
                    b = (a + 2) % RING
                    pe.wait_ge(s_slot[b], 16 * (i + 1 if b == a + 2 else i + 2))
                    wait(pe, s_sl, n + 2)
                    nc.tensor.transpose(ps_slot[:, 0:P], slot_rows[:, b, 0:D], idn).then_inc(s_sT, 1)
                if live(n - 1, FTILES):
                    b = (a - 1) % RING
                    at = pe.snap(before * D)
                    pe.wait_ge(s_hTr, n)
                    wait(pe, s_yb, n - 2)
                    for c in range(FC):
                        last = nc.tensor.matmul(ps_y[b % 2][:, 0:D], hT[:, b % 2, c, :],
                                                w2_all[:, c, :, :].rearrange("p e d -> p (e d)")[:, bass.ds(at, D)],
                                                start=(c == 0), stop=(c == FC - 1))
                    last.then_inc(s_down, 1)

            slot_tiles(pe, slot_tile, groups=group_experts)


_INS = ['x', 'L0_tok_pos_table', 'L0_tok_nest_table', 'L0_tok_seg_table', 'L0_tok_W', 'L0_attn_w_qkv',
        'L0_attn_w_out', 'L0_attn_b_out', 'L0_attn_proj', 'L0_ffn_Wg', 'L0_ffn_bg', 'L0_ffn_W1', 'L0_ffn_b1',
        'L0_ffn_W2', 'L0_ffn_b2']
_OUT = (16, 256, 128)


def kernel(**inputs):
    import numpy as _np
    import concourse.bacc as _bacc
    from concourse import mybir as _mybir
    from concourse.bass_utils import run_bass_kernel_spmd as _run

    nc = _bacc.Bacc("TRN2", target_bir_lowering=False, num_devices=1)
    arrays, args = {}, []
    for name in _INS:
        a = _np.ascontiguousarray(inputs[name])
        arrays[f"in_{name}"] = a
        args.append(nc.dram_tensor(f"in_{name}", a.shape, _mybir.dt.from_np(a.dtype), kind="ExternalInput").ap())
    args.append(nc.dram_tensor("out", _OUT, _mybir.dt.float32, kind="ExternalOutput").ap())
    lm_tower_kernel(nc, *args)
    r = _run(nc, [arrays], core_ids=[0])
    return r.results[0]["out"]
```

```python
from contextlib import ExitStack

import concourse.bass as bass
from concourse import mybir


class Steps:

    def __init__(self, eng, sem):
        self.eng, self.sem, self.base, self.count = eng, sem, 0, 0

    def done(self, instruction):
        self.add(instruction)
        self.wait()

    def add(self, instruction):
        instruction.then_inc(self.sem, 1)
        self.count += 1

    def wait(self):
        self.eng.wait_ge(self.sem, self.base + self.count)


def span(start, size):
    return slice(start, start + size) if isinstance(start, int) else bass.ds(start, size)


def wait(eng, sem, count):
    if not isinstance(count, int) or count > 0:
        eng.wait_ge(sem, count)


def lm_tower_kernel(nc, x, pos_table, nest_table, seg_table, tok_w, w_qkv, w_out, b_out, proj,
                    w_gate, b_gate, w_one, b_one, w_two, b_two, out):
    f32 = mybir.dt.float32
    f32r = mybir.dt.float32r
    bf16 = mybir.dt.bfloat16
    i32 = mybir.dt.int32
    u32 = mybir.dt.uint32
    ALU = mybir.AluOpType
    ACT = mybir.ActivationFunctionType
    AX = mybir.AxisListType

    B, S = x.shape
    P = 128
    D = tok_w.shape[1]
    SEQS = B
    TILES = B * S // P
    HEADS, DH = 8, 64
    HC = HEADS // 2
    HD = HEADS * DH
    NNEST, NSEG = nest_table.shape[0], seg_table.shape[0]
    E = w_gate.shape[1]
    E_BITS = (E - 1).bit_length()
    FF = w_one.shape[2]
    FC = FF // P
    TOP = 2
    LN_EPS, D_EPS, TOP_EPS = 1e-5, 1e-4, 0.01
    SLOT = 32
    PARTS = 3
    TR = SLOT * PARTS

    CHOICES = TOP * B * S
    CAP = B * S + P
    FTILES = CHOICES // P + E
    EMPTY = E * CAP
    EMPTIES = FTILES - CHOICES // P
    SLOTS = EMPTY + EMPTIES * P
    ROW = D + 2 * E
    PLACES = CHOICES + E * P + EMPTIES * P

    L0, L1 = 4, SEQS - 2
    LAST = (SEQS - 2, SEQS - 1)
    HEAD_SEQS = 2
    RING = 6
    DIGITS = RING + 3
    LOW_DIGITS = 24 // E_BITS

    def live(n, count=SEQS):
        return not isinstance(n, int) or 0 <= n < count

    def sequences(eng, step, body, per=None):
        for p in range(-2, L0):
            body(p, p % 2, p // 2)
        start = step.base + step.count if step else 0
        with eng.Fori(0, (L1 - L0) // 2) as i:
            if step:
                step.base, step.count = start + i * per, 0
            for a in range(2):
                body(2 * i + L0 + a, a, i + L0 // 2)
            if step:
                assert step.count == per, step.count
        if step:
            step.base, step.count = start + per * ((L1 - L0) // 2), 0
        for p in range(L1, SEQS + 3):
            body(p, p % 2, p // 2)

    def slot_tiles(eng, body, step=None, per=None, groups=None):
        def load(group):
            if groups is None:
                return [None] * DIGITS
            word = eng.value_load(groups[0:1, span(group, 1)], min_val=0, max_val=E ** DIGITS - 1)
            return [eng.snap((word >> (E_BITS * k)) & (E - 1)) for k in range(DIGITS)]

        values = load(0)
        for n in range(-3, RING):
            body(n, n % RING, n // RING, values[max(n, 0)], values[n + 3])
        start = step.base + step.count if step else 0
        with eng.Fori(1, FTILES // RING - 1) as i:
            values = load(i)
            if step:
                step.base, step.count = start + (i - 1) * per, 0
            for a in range(RING):
                body(i * RING + a, a, i, values[a], values[a + 3])
            if step:
                assert step.count == per, step.count
        if step:
            step.base, step.count = start + per * (FTILES // RING - 2), 0
        first = FTILES - RING
        values = load(FTILES // RING - 1)
        for n in range(first, FTILES + 2):
            body(n, n % RING, n // RING, values[n - first], values[min(n - first + 3, DIGITS - 1)])

    ctx = ExitStack()
    with ctx:
        def sb(name, shape, dt=f32):
            return ctx.enter_context(nc.sbuf_tensor(name, shape, dt))

        def pb(name, shape):
            return ctx.enter_context(nc.psum_tensor(name, shape, f32))

        def sem(name):
            return ctx.enter_context(nc.semaphore(name))

        ident = sb("ident", [P, P])
        before = sb("before", [P, P], bf16)
        ones = sb("ones", [P, P], bf16)
        part_ones = sb("part_ones", [TR, P], bf16)
        minus_half = sb("minus_half", [P, 2])
        ln_eps = sb("ln_eps", [P, 2])
        spare = sb("spare", [P, 2])
        zero = sb("zero", [P, 2])
        one = sb("one", [P, 2])
        minus_one = sb("minus_one", [P, 2])
        top_eps = sb("top_eps", [P, 2])
        second = sb("second", [P, E])
        table_id = sb("table_id", [TR, 1])
        expert_id = sb("expert_id", [P, E])
        expert_at = sb("expert_at", [P, E + 1])
        token_id = sb("token_id", [P, TILES])
        tile_id = sb("tile_id", [P, FTILES])
        pad_rows = sb("pad_rows", [P, E, ROW])
        empty_rows = sb("empty_rows", [P, EMPTIES, ROW])

        tok_rows = sb("tok_rows", [P, 3, D])
        pos_rows = sb("pos_rows", [P, 2, D])
        nest_rows = sb("nest_rows", [TR, D])
        seg_rows = sb("seg_rows", [TR, D])
        bias_rows = sb("bias_rows", [TR, D])
        proj_diag = sb("proj_diag", [P, P])
        qkv_rows = sb("qkv_rows", [P, 3 * HC, D])
        out_rows = sb("out_rows", [P, HD])
        gate_w = sb("gate_w", [P, E])
        gate_b = sb("gate_b", [P, E])
        w1_all = sb("w1_all", [P, E, FF])
        w1_hi = sb("w1_hi", [P, E * FF], f32r)
        w1_lo = sb("w1_lo", [P, E * FF], f32r)
        w2_all = sb("w2_all", [P, FC, E, D])
        b1_all = sb("b1_all", [P, E * FF])
        b2_all = sb("b2_all", [P, E * D])
        rows_T = sb("rows_T", [P, 2 * P + 2 * TR])
        proj_T = sb("proj_T", [P, P])
        out_w = sb("out_w", [P, HC, D])
        pos_part = sb("pos_part", [P, 2, D])
        split_hi = sb("split_hi", [TR, 2, D], bf16)
        split_mid = sb("split_mid", [TR, 2, D], bf16)
        split_lo = sb("split_lo", [TR, 2, D], bf16)
        rest_one = sb("rest_one", [TR, 2, D])
        rest_two = sb("rest_two", [TR, 2, D])
        table = sb("table", [TR, 2, D], bf16)
        qkv_hi = sb("qkv_hi", [P, 3, HD], f32r)
        qkv_lo = sb("qkv_lo", [P, 3, HD], f32r)

        tokens = sb("tokens", [B, S], i32)
        zeros = sb("zeros", [B, S])
        delta = sb("delta", [B, S])
        other = sb("other", [B, S])
        depth = sb("depth", [B, S])
        floor = sb("floor", [B, S])
        nesting = sb("nesting", [B, S], bf16)
        seg_count = sb("seg_count", [B, S], i32)
        seg_int = sb("seg_int", [B, S], i32)
        segments = sb("segments", [B, S], bf16)
        row_of = sb("row_of", [TR, B * S], bf16)
        one_hot = sb("one_hot", [TR, 2, S], bf16)

        stats = sb("stats", [P, 2, 6])
        moments = sb("moments", [P, 2, 2, 2])
        rstd = sb("rstd", [P, 2, 2])
        shift = sb("shift", [P, 2, 2])
        xhat = sb("xhat", [P, 2, 2, D])
        xT_hi = sb("xT_hi", [P, 2, S], f32r)
        xT_lo = sb("xT_lo", [P, 2, S], f32r)

        qk_max = sb("qk_max", [P, 2, HEADS])
        q_prime = sb("q_prime", [P, 2, HD])
        k_prime = sb("k_prime", [P, 2, HD])
        v_ones = sb("v_ones", [P, 2, HEADS, DH + 1])
        context = sb("context", [P, 2, HC, 2, DH + 1])
        qT = sb("qT", [P, 2, HC, P])
        d_sum = sb("d_sum", [P, HEADS])
        d_inv = sb("d_inv", [P, HEADS])
        heads_out = sb("heads_out", [P, 2, HD])
        oT = sb("oT", [P, 2, HC, P])
        h = sb("h", [P, TILES, D])

        stats2 = sb("stats2", [P, 2, 6])
        moments2 = sb("moments2", [P, 2, 2, 2])
        rstd2 = sb("rstd2", [P, 2, 2])
        shift2 = sb("shift2", [P, 2, 2])
        rows = sb("rows", [P, 3, 2, ROW])
        x2T = sb("x2T", [P, 2, S])
        logits = sb("logits", [P, 2, E])
        top = sb("top", [P, 2, E])
        top_id = sb("top_id", [P, 2, E], u32)
        below = sb("below", [P, 2, E])
        exps = sb("exps", [P, 2, E])
        chosen = sb("chosen", [P, 2, TOP, E])
        chosen_w = sb("chosen_w", [P, 2, TOP, E])
        chosen_at = sb("chosen_at", [P, 2, TOP, E])
        mask = sb("mask", [P, 2, E], bf16)
        last_denom = sb("last_denom", [P, 2])
        last_weight = sb("last_weight", [P, 2, TOP])
        last_chosen_w = sb("last_chosen_w", [P, 2, TOP, E])
        partial = sb("partial", [P, 2, E])
        denom = sb("denom", [P, 2])
        second_at = sb("second_at", [P, 2, E])
        weight = sb("weight", [P, 2, TOP])
        next_row = sb("next_row", [P, E])
        row_at = sb("row_at", [P, 2, E])
        row_id = sb("row_id", [P, 3, 2, TOP], i32)

        rows_used = sb("rows_used", [P, E])
        rows_up = sb("rows_up", [P, E], i32)
        tiles_of = sb("tiles_of", [P, E], i32)
        tiles_to = sb("tiles_to", [P, E])
        shift_at = sb("shift_at", [P, E + 1])
        shift_by = sb("shift_by", [P, E])
        past = qT[:, :, :, :].rearrange("p a c t -> p (a c t)")[:, 0:FTILES * E].rearrange("p (n e) -> p n e", e=E)
        past_by = oT[:, :, :, :].rearrange("p a c t -> p (a c t)")[:, 0:FTILES * E].rearrange("p (n e) -> p n e", e=E)
        expert_f = sb("expert_f", [P, FTILES])
        first_f = sb("first_f", [P, FTILES])
        tile_expert = sb("tile_expert", [P, FTILES + 2 * RING])
        digit = sb("digit", [P, RING])
        digits = sb("digits", [P, FTILES // RING, RING])
        low_word = sb("low_word", [P, FTILES // RING], i32)
        high_digit = sb("high_digit", [P, FTILES // RING], i32)
        group_f = sb("group_f", [P, FTILES // RING])
        group_experts = sb("group_experts", [P, FTILES // RING], i32)
        tile_row = sb("tile_row", [P, FTILES], i32)
        pad_at = sb("pad_at", [P, E], i32)

        spent = qkv_rows[:, :, :].rearrange("p a c -> p (a c)")
        slot_rows = spent[:, 0:RING * ROW].rearrange("p (a r) -> p a r", a=RING)
        y = heads_out[:, :, :].rearrange("p a c -> p (a c)")[:, 0:RING * D].rearrange("p (a d) -> p a d", a=RING)
        sT_hi, sT_lo = xT_hi[:, :, 0:P], xT_lo[:, :, 0:P]
        hidden = q_prime[:, :, :]
        hT = k_prime[:, :, :].rearrange("p a (c t) -> p a c t", c=FC)
        y_biased = spent[:, RING * ROW:RING * ROW + 2 * D].rearrange("p (a d) -> p a d", a=2)
        slot_w = sb("slot_w", [P, RING, 1])
        place = sb("place", [P, RING, 1], i32)

        Y_TILES = 4
        y_first = w1_all[:, :, :].rearrange("p e (t d) -> p (e t) d", d=D)
        y_second = b1_all[:, :].rearrange("p (t d) -> p t d", d=D)

        ps_q = pb("ps_q", [P, HD])
        ps_k = pb("ps_k", [P, HD])
        ps_vc = pb("ps_vc", [P, HD])
        ps_qT = pb("ps_qT", [P, HD])
        ps_out = pb("ps_out", [P, 2, HD])
        ps_oy = pb("ps_oy", [P, HD])
        ps_ln = pb("ps_ln", [P, HD])
        ps_ctx = ps_vc[:, 0:HC * (DH + 1)].rearrange("p (c d) -> p c d", c=HC)
        ps_slot, ps_up, ps_hT, ps_y = ps_ln, (ps_q, ps_k), ps_qT, (ps_oy, ps_vc)

        ids_dram = nc.dram_tensor("ids_dram", [2, B, S], bf16)
        slots_dram = nc.dram_tensor("slots_dram", [SLOTS, ROW], f32)
        y_dram = nc.dram_tensor("y_dram", [PLACES, D], f32)

        s_tok = sem("tokens_in")
        s_emb_w = sem("embedding_weights_in")
        s_att_w = sem("attention_weights_in")
        s_bias_w = sem("out_bias_in")
        s_gate_w = sem("gate_weights_in")
        s_w1 = sem("w1_in")
        s_ffn_w = sem("ffn_weights_in")
        s_zero = sem("rows_zeroed")
        s_ident = sem("ident_made")
        s_const = sem("constants_made")
        s_vec = sem("vector_chain")
        s_pool = sem("pool_chain")
        s_ids = sem("ids_made")
        s_ids_out = sem("ids_in_dram")
        s_row_head, s_row = sem("first_rows_in"), sem("rows_in")
        s_t1 = sem("setup_transposed")
        s_t1c = sem("setup_copied")
        s_wT = sem("weight_products")
        s_wTc = sem("weight_products_split")
        s_hi = sem("weight_highs")
        s_ctx0 = sem("context_zeroed")

        s_hot = sem("one_hot_ready")
        s_emb = sem("embedding_done")
        s_h = sem("h_ready")
        s_mom, s_rstd = sem("moments_ready"), sem("rstd_ready")
        s_xhat = sem("xhat_ready")
        s_xT = sem("xT_done")
        s_xh, s_xl = sem("xT_hi_ready"), sem("xT_lo_ready")
        s_q, s_k, s_v = sem("q_done"), sem("k_done"), sem("v_done")
        s_qs, s_ks = sem("q_shifted"), sem("k_shifted")
        s_qp, s_kp, s_vo = sem("q_prime_ready"), sem("k_prime_ready"), sem("v_ready")
        s_c, s_cr = sem("context_done"), sem("context_ready")
        s_qT, s_qTr = sem("qT_done"), sem("qT_ready")
        s_o, s_or = sem("out_done"), sem("heads_out_ready")
        s_oT, s_oTr = sem("oT_done"), sem("oT_ready")
        s_y, s_h2 = sem("y_done"), sem("h2_ready")
        s_mom2, s_rstd2 = sem("moments2_ready"), sem("rstd2_ready")
        s_xhat2 = sem("xhat2_ready")
        s_x2T, s_x2Tr = sem("x2T_done"), sem("x2T_ready")
        s_lg, s_lgr = sem("logits_done"), sem("logits_read")
        s_below, s_exps = sem("logits_below_top"), sem("gate_exps_ready")
        s_mask = sem("mask_ready")
        s_rank, s_rankr = sem("ranks_done"), sem("ranks_read")
        s_id = sem("row_ids_ready")
        s_weighed, s_last_weighed = sem("weights_ready"), sem("last_weights_ready")
        s_slots = [sem(f"rows_in_slots{a}") for a in range(2)]
        s_w1h, s_w1l = sem("w1_hi_ready"), sem("w1_lo_ready")
        s_empty = sem("empty_rows_in_slots")
        s_tiles = sem("slot_tiles_known")
        s_groups = sem("group_experts_known")
        s_pad_at = sem("padding_places_known")
        s_pad = sem("padding_in_slots")

        s_slot = [sem(f"slot_rows_in{a}") for a in range(RING)]
        s_sT, s_sh, s_sl = sem("slots_T_done"), sem("slots_T_hi_ready"), sem("slots_T_lo_ready")
        s_up, s_hid = sem("up_done"), sem("hidden_ready")
        s_hT, s_hTr = sem("hidden_T_done"), sem("hidden_T_ready")
        s_down, s_yb = sem("down_done"), sem("y_biased_ready")
        s_meta, s_yr = sem("slot_weights_ready"), sem("y_ready")
        s_placed = [sem(f"y_in_dram{a}") for a in range(RING)]
        s_back = [sem(f"y_in{c}") for c in range(TILES // Y_TILES)]
        s_tot = sem("total_ready")
        s_out = sem("out_written")

        block = ctx.enter_context(nc.Block())

        EMB_DMAS, ATT_DMAS, FFN_DMAS, GATE_DMAS = 8, 4, 3, 2

        def pad(eng, half):
            eng.wait_ge(s_pad_at, 1)
            for e in range(half, E, 2):
                at = eng.value_load(pad_at[0:1, e:e + 1], min_val=0, max_val=EMPTY - P)
                eng.dma_start(slots_dram[bass.ds(at, P), :], pad_rows[:, e, :]).then_inc(s_pad, 16)

        def place_of(p, a):
            return 2 if isinstance(p, int) and p == SEQS - 1 else a

        def weighed(eng, p):
            if isinstance(p, int) and p in LAST:
                eng.wait_ge(s_last_weighed, p - LAST[0] + 1)
            else:
                wait(eng, s_weighed, p + 1)

        def load_tables(eng, r):
            eng.dma_start(nest_rows[SLOT * r:SLOT * r + NNEST, :], nest_table[:, :]).then_inc(s_emb_w, 16)
            eng.dma_start(seg_rows[SLOT * r + NNEST:SLOT * r + NNEST + NSEG, :], seg_table[:, :]).then_inc(s_emb_w, 16)

        @block.sync
        def _(sp):
            sp.dma_start(tokens[:, :], x[:, :]).then_inc(s_tok, 16)
            sp.dma_start(tok_rows[:, :, :], tok_w.rearrange("(a p) h -> p a h", p=P)).then_inc(s_emb_w, 16)
            sp.dma_start(pos_rows[:, :, :], pos_table[0:S, :].rearrange("(a p) h -> p a h", p=P)).then_inc(s_emb_w, 16)
            sp.wait_ge(s_zero, 1)
            load_tables(sp, 0)
            load_tables(sp, 1)
            for r in range(PARTS):
                sp.dma_start(bias_rows[SLOT * r:SLOT * r + 1, :], b_out.rearrange("(o d) -> o d", o=1))\
                    .then_inc(s_bias_w, 16)
            sp.wait_ge(s_ids, 1)
            sp.dma_start(ids_dram[1, :, :], segments[:, :]).then_inc(s_ids_out, 16)
            sp.wait_ge(s_ids, 2)
            sp.dma_start(ids_dram[0, :, :], nesting[:, :]).then_inc(s_ids_out, 16)
            sp.wait_ge(s_ids_out, 32)
            for first, last, done in ((0, HEAD_SEQS, s_row_head), (HEAD_SEQS, B, s_row)):
                for r in range(PARTS):
                    sp.dma_start(row_of[SLOT * r:SLOT * r + SLOT, first * S:last * S],
                                 ids_dram[:, first:last, :].rearrange("(k o) b s -> k o (b s)", o=1)
                                 .to_broadcast([2, SLOT // 2, (last - first) * S])).then_inc(done, 16)
            sp.dma_start(w1_all[:, :, :], w_one.rearrange("e d f -> d e f")).then_inc(s_w1, 16)
            sp.dma_start(b1_all[:, :], b_one.rearrange("(o e) f -> o (e f)", o=1).to_broadcast([P, E * FF]))\
                .then_inc(s_ffn_w, 16)
            sp.dma_start(b2_all[:, :], b_two.rearrange("(o e) d -> o (e d)", o=1).to_broadcast([P, E * D]))\
                .then_inc(s_ffn_w, 16)
            for e in range(E):
                sp.dma_start(w2_all[:, :, e, :], w_two[e, :, :].rearrange("(c p) d -> p c d", p=P)).then_inc(s_ffn_w, 16)
            sp.wait_ge(s_const, 1)
            sp.dma_start(slots_dram[EMPTY:SLOTS, :].rearrange("(n p) r -> p n r", p=P), empty_rows[:, :, :])\
                .then_inc(s_empty, 16)

            pad(sp, 0)
            sp.wait_ge(s_tiles, 1)
            firsts = [sp.value_load(tile_row[0:1, n:n + 1], min_val=0, max_val=SLOTS - P) for n in range(RING)]
            sp.wait_ge(s_pad, 16 * E)
            sp.wait_ge(s_empty, 16)
            for a in range(2):
                sp.wait_ge(s_slots[a], 16 * 2 * TOP * SEQS // 2)
            for n in range(RING):
                sp.dma_start(slot_rows[:, n, :], slots_dram[bass.ds(firsts[n], P), :]).then_inc(s_slot[n], 16)

            def load_ahead(n, a, i, before, after):
                if live(n, FTILES) and live(n + RING, FTILES):
                    sp.wait_ge(s_meta, n + 1)
                    at = sp.value_load(tile_row[0:1, span(n + RING, 1)], min_val=0, max_val=SLOTS - P)
                    sp.dma_start(slot_rows[:, a, :], slots_dram[bass.ds(at, P), :]).then_inc(s_slot[a], 16)

            slot_tiles(sp, load_ahead)

            for a in range(RING):
                sp.wait_ge(s_placed[a], 16 * FTILES // RING)
            for c in range(TILES // Y_TILES):
                at = c * Y_TILES * P
                for k, dst in enumerate((y_first, y_second)):
                    sp.dma_start(dst[:, c * Y_TILES:c * Y_TILES + Y_TILES, :],
                                 y_dram[k * B * S + at:k * B * S + at + Y_TILES * P, :]
                                 .rearrange("(j p) d -> p j d", p=P)).then_inc(s_back[c], 16)

        @block.gpsimd
        def _(pool):
            step = Steps(pool, s_pool)
            nc.gpsimd.memset(nest_rows[:, :], 0.0)
            nc.gpsimd.memset(seg_rows[:, :], 0.0)
            nc.gpsimd.memset(bias_rows[:, :], 0.0)
            nc.gpsimd.memset(proj_diag[:, :], 0.0).then_inc(s_zero, 1)
            step.done(nc.gpsimd.memset(ident[:, :], 0.0))
            nc.gpsimd.affine_select(out=ident[:, :], in_=ident[:, :], compare_op=ALU.not_equal, fill=1.0, base=0,
                                    pattern=[[-1, P]], channel_multiplier=1).then_inc(s_ident, 1)
            nc.gpsimd.memset(minus_half[:, :], -0.5)
            nc.gpsimd.memset(ln_eps[:, :], LN_EPS)
            nc.gpsimd.memset(zero[:, :], 0.0)
            nc.gpsimd.memset(one[:, :], 1.0)
            nc.gpsimd.memset(minus_one[:, :], -1.0)
            nc.gpsimd.memset(top_eps[:, :], TOP_EPS)
            nc.gpsimd.memset(second[:, :], float(B * S))
            for r in range(PARTS):
                step.done(nc.gpsimd.iota(table_id[SLOT * r:SLOT * r + SLOT, :], [[0, 1]], base=0, channel_multiplier=1,
                                         allow_small_or_imprecise_dtypes=True))
            step.done(nc.gpsimd.memset(part_ones[:, :], 0.0))
            for r in range(PARTS):
                step.done(nc.gpsimd.memset(part_ones[SLOT * r:SLOT * r + 1, :], 1.0))
            nc.gpsimd.memset(context[:, :, :, :, :], 0.0).then_inc(s_ctx0, 1)
            for a in range(2):
                nc.gpsimd.memset(v_ones[:, a, :, DH:DH + 1], 1.0).then_inc(s_ctx0, 1)
            nc.gpsimd.memset(ones[:, :], 1.0)
            for r in range(RING):
                nc.gpsimd.memset(digit[:, r:r + 1], float(E ** r))
            step.done(nc.gpsimd.memset(before[:, :], 1.0))
            nc.gpsimd.affine_select(out=before[:, :], in_=before[:, :], compare_op=ALU.is_gt, fill=0.0, base=0,
                                    pattern=[[1, P]], channel_multiplier=-1)
            nc.gpsimd.iota(expert_id[:, :], [[1, E]], base=0, channel_multiplier=0,
                           allow_small_or_imprecise_dtypes=True)
            nc.gpsimd.iota(expert_at[:, :], [[CAP, E + 1]], base=0, channel_multiplier=0,
                           allow_small_or_imprecise_dtypes=True)
            nc.gpsimd.iota(next_row[:, :], [[CAP, E]], base=0, channel_multiplier=0,
                           allow_small_or_imprecise_dtypes=True)
            nc.gpsimd.iota(token_id[:, :], [[P, TILES]], base=0, channel_multiplier=1,
                           allow_small_or_imprecise_dtypes=True)
            nc.gpsimd.iota(tile_id[:, :], [[1, FTILES]], base=0, channel_multiplier=0,
                           allow_small_or_imprecise_dtypes=True)
            step.add(nc.gpsimd.memset(pad_rows[:, :, :], 0.0))
            step.done(nc.gpsimd.memset(empty_rows[:, :, :], 0.0))
            nc.gpsimd.iota(pad_rows[:, :, D + E:ROW], [[P, E], [0, E]], base=CHOICES, channel_multiplier=1,
                           allow_small_or_imprecise_dtypes=True)
            nc.gpsimd.iota(empty_rows[:, :, D + E:ROW], [[P, EMPTIES], [0, E]], base=CHOICES + E * P,
                           channel_multiplier=1, allow_small_or_imprecise_dtypes=True).then_inc(s_const, 1)

            def take_wait():
                step.wait()
                step.add(nc.gpsimd.tensor_tensor(spare[:, :], minus_half[:, :], ln_eps[:, :], ALU.add))

            def scale_and_shift(p, a, mom, rs, sh, mom_sem, out_sem):
                pool.wait_ge(mom_sem, p + 1)
                step.done(nc.gpsimd.tensor_tensor(rs[:, a, :], mom[:, a, :, 1], ln_eps[:, :], ALU.add))
                step.done(nc.gpsimd.tensor_tensor(rs[:, a, :], rs[:, a, :], minus_half[:, :], ALU.pow))
                step.done(nc.gpsimd.tensor_tensor(sh[:, a, :], mom[:, a, :, 0], rs[:, a, :], ALU.mult))
                nc.gpsimd.tensor_tensor(sh[:, a, :], zero[:, :], sh[:, a, :], ALU.subtract).then_inc(out_sem, 1)

            def weigh(p, a):
                pool.wait_ge(s_exps, p + 1)
                terms, width = exps, E // 2
                while width:
                    step.done(nc.gpsimd.tensor_tensor(partial[:, :, 0:width], terms[:, :, 0:width],
                                                      terms[:, :, width:2 * width], ALU.add))
                    terms, width = partial, width // 2
                step.done(nc.gpsimd.tensor_tensor(denom[:, :], partial[:, :, 0], top_eps[:, :], ALU.mult))
                step.done(nc.gpsimd.tensor_tensor(denom[:, :], denom[:, :], exps[:, :, 1], ALU.add))
                step.done(nc.gpsimd.tensor_tensor(denom[:, :], denom[:, :], one[:, :], ALU.add))
                step.done(nc.gpsimd.tensor_tensor(weight[:, :, 0], denom[:, :], minus_one[:, :], ALU.pow))
                pool.wait_ge(s_mask, p + 1)
                step.add(nc.gpsimd.tensor_tensor(second_at[:, :, :], chosen[:, :, 1, :],
                                                 second[:, None, :].to_broadcast([P, 2, E]), ALU.mult))
                step.done(nc.gpsimd.tensor_tensor(weight[:, :, 1], weight[:, :, 0], exps[:, :, 1], ALU.mult))
                nc.gpsimd.tensor_tensor(rows[:, place_of(p, a), :, D + E:ROW], second_at[:, :, :],
                                        token_id[:, span(2 * p, 2), None].to_broadcast([P, 2, E]), ALU.add)
                step.done(nc.gpsimd.tensor_tensor(chosen_w[:, :, :, :], chosen[:, :, :, :],
                                                  weight[:, :, :, None].to_broadcast([P, 2, TOP, E]), ALU.mult))
                nc.gpsimd.tensor_tensor(rows[:, place_of(p, a), :, D:D + E], chosen_w[:, :, 0, :], chosen_w[:, :, 1, :],
                                        ALU.add).then_inc(s_weighed, 1)

            def scatter(p, a):
                pool.wait_ge(s_id, p + 1)
                take_wait()
                for j in range(2):
                    for k in range(TOP):
                        nc.gpsimd.indirect_dma_start(
                            slots_dram[:, :], bass.IndirectOffsetOnAxis(row_id[:, place_of(p, a), j, k:k + 1], 0),
                            rows[:, place_of(p, a), j, :], None).then_inc(s_slots[a], 16)

            def sequence(p, a, half):
                if live(p - 3):
                    if isinstance(p, int) and p - 3 in LAST:
                        pool.wait_ge(s_last_weighed, p - 3 - LAST[0] + 1)
                    else:
                        weigh(p - 3, 1 - a)
                        if isinstance(p, int) and p == SEQS:
                            scale_and_shift(p - 1, 1 - a, moments2, rstd2, shift2, s_mom2, s_rstd2)
                        pool.wait_ge(s_weighed, p - 2)
                    scatter(p - 3, 1 - a)
                if live(p + 2):
                    scale_and_shift(p + 2, a, moments, rstd, shift, s_mom, s_rstd)
                if live(p - 1) and not (isinstance(p, int) and p == SEQS):
                    scale_and_shift(p - 1, 1 - a, moments2, rstd2, shift2, s_mom2, s_rstd2)
                if live(p):
                    pool.wait_ge(s_w1h, p + 1)
                    at = span(p * (E * FF // SEQS), E * FF // SEQS)
                    nc.gpsimd.tensor_tensor(w1_lo[:, at], w1_all[:, :, :].rearrange("p e f -> p (e f)")[:, at],
                                            w1_hi[:, at].bitcast(f32), ALU.subtract).then_inc(s_w1l, 1)

            sequences(pool, step, sequence, 34)

            def place_y(n, a, i, before, after):
                if live(n, FTILES):
                    pool.wait_ge(s_yr, n + 1)
                    take_wait()
                    nc.gpsimd.indirect_dma_start(
                        y_dram[:, :], bass.IndirectOffsetOnAxis(place[:, a, :], 0),
                        y[:, a, :], None).then_inc(s_placed[a], 16)

            slot_tiles(pool, place_y, step, RING)

        @block.scalar
        def _(act):
            act.dma_start(qkv_rows[:, :, :], w_qkv.rearrange("(a p) c -> p a c", p=P)).then_inc(s_att_w, 16)
            act.dma_start(out_rows[:, :], w_out[:, :]).then_inc(s_att_w, 16)
            act.wait_ge(s_zero, 1)
            load_tables(act, 2)
            for r in range(2):
                act.dma_start(proj_diag[DH * r:DH * r + DH, DH * r:DH * r + DH], proj[:, :]).then_inc(s_att_w, 16)
            act.dma_start(gate_w[:, :], w_gate[:, :]).then_inc(s_gate_w, 16)
            act.dma_start(gate_b[:, :], b_gate.rearrange("(o d) -> o d", o=1).to_broadcast([P, E])).then_inc(s_gate_w, 16)
            act.wait_ge(s_t1, 1)
            nc.scalar.activation(rows_T[:, :], ps_q[:, 0:2 * P + 2 * TR], ACT.Copy).then_inc(s_t1c, 1)
            act.wait_ge(s_t1, 2)
            nc.scalar.activation(proj_T[:, :], ps_k[:, 0:P], ACT.Copy).then_inc(s_t1c, 1)
            act.wait_ge(s_t1, 3)
            nc.scalar.activation(out_w[:, :, :], ps_qT[:, :], ACT.Copy).then_inc(s_hi, 1)
            act.wait_ge(s_t1, 4)
            nc.scalar.activation(qkv_hi[:, 2, :], ps_vc[:, :], ACT.Copy).then_inc(s_hi, 1)
            act.wait_ge(s_wT, 2)
            nc.scalar.activation(qkv_hi[:, 0, :], ps_out[:, 0, :], ACT.Copy, scale=DH ** -0.5).then_inc(s_hi, 1)
            act.wait_ge(s_wT, 3)
            nc.scalar.activation(qkv_hi[:, 1, :], ps_out[:, 1, :], ACT.Copy).then_inc(s_hi, 1)

            def xT_high(p, a):
                act.wait_ge(s_xT, p + 1)
                wait(act, s_v, 2 * p - 2)
                nc.scalar.activation(xT_hi[:, a, :], ps_ln[:, 0:S], ACT.Copy).then_inc(s_xh, 1)

            def q_exp(t, a):
                act.wait_ge(s_qs, t + 1)
                nc.scalar.activation(q_prime[:, a, :], q_prime[:, a, :], ACT.Exp).then_inc(s_qp, 1)

            def k_exp(t, a):
                act.wait_ge(s_ks, t + 1)
                nc.scalar.activation(k_prime[:, a, :], k_prime[:, a, :], ACT.Exp).then_inc(s_kp, 1)

            def v_copy(t, a):
                act.wait_ge(s_v, t + 1)
                wait(act, s_c, t - 1)
                nc.scalar.activation(v_ones[:, a, :, 0:DH], ps_vc[:, :].rearrange("p (h d) -> p h d", h=HEADS),
                                     ACT.Copy).then_inc(s_vo, 1)

            def qT_copy(t, a):
                act.wait_ge(s_qT, t + 1)
                wait(act, s_o, t - 1)
                nc.scalar.activation(qT[:, a, :, :], ps_qT[:, :], ACT.Copy).then_inc(s_qTr, 1)

            def context_copy(t, a):
                act.wait_ge(s_c, t + 1)
                nc.scalar.activation(context[0:DH, a, :, 0, :], ps_ctx[0:DH], ACT.Copy)
                nc.scalar.activation(context[DH:P, a, :, 1, :], ps_ctx[DH:P], ACT.Copy).then_inc(s_cr, 1)

            def oT_copy(t, a):
                act.wait_ge(s_oT, t + 1)
                nc.scalar.activation(oT[:, a, :, :], ps_oy[:, :], ACT.Copy).then_inc(s_oTr, 1)

            def x2T_copy(p, a):
                act.wait_ge(s_x2T, p + 1)
                nc.scalar.activation(x2T[:, a, :], ps_ln[:, 0:S], ACT.Copy).then_inc(s_x2Tr, 1)

            def w1_high(p):
                if isinstance(p, int) and p == 0:
                    act.wait_ge(s_w1, 16)
                at = span(p * (E * FF // SEQS), E * FF // SEQS)
                nc.scalar.activation(w1_hi[:, at], w1_all[:, :, :].rearrange("p e f -> p (e f)")[:, at],
                                     ACT.Copy).then_inc(s_w1h, 1)

            def normalize(p, a, rs, sh, dst, rstd_sem, out_sem):
                act.wait_ge(rstd_sem, p + 1)
                for k in range(2):
                    last = nc.scalar.activation(dst(k), h[:, span(2 * p + k, 1), :].rearrange("p o d -> p (o d)"),
                                                ACT.Identity, bias=sh[:, a, k:k + 1], scale=rs[:, a, k:k + 1])
                last.then_inc(out_sem, 1)

            def sequence(p, a, half):
                for j in range(2):
                    t = 2 * p + j
                    if j == 1 and live(p - 2):
                        x2T_copy(p - 2, a)
                    if live(p):
                        context_copy(t, j)
                    if live(t - 1, TILES):
                        oT_copy(t - 1, 1 - j)
                    if live(t + 1, TILES):
                        q_exp(t + 1, 1 - j)
                    if j == 0 and live(p + 1):
                        xT_high(p + 1, 1 - a)
                    if live(t + 1, TILES):
                        k_exp(t + 1, 1 - j)
                    if j == 0 and live(p - 2):
                        if place_of(p - 2, a) == a:
                            wait(act, s_slots[a], 16 * 2 * TOP * (half - 1))
                        normalize(p - 2, a, rstd2, shift2, lambda k: rows[:, place_of(p - 2, a), k, 0:D], s_rstd2, s_xhat2)
                    if live(t + 1, TILES):
                        v_copy(t + 1, 1 - j)
                    if live(t + 1, TILES):
                        qT_copy(t + 1, 1 - j)
                    if j == 1 and live(p - 2):
                        act.wait_ge(s_below, p - 1)
                        weighed(act, p - 3)
                        nc.scalar.activation(exps[:, :, :], below[:, :, :], ACT.Exp).then_inc(s_exps, 1)
                    if j == 1 and live(p + 2):
                        wait(act, s_xT, p + 1)
                        normalize(p + 2, a, rstd, shift, lambda k: xhat[:, a, k, :], s_rstd, s_xhat)
                    if j == 1 and live(p):
                        w1_high(p)

            act.wait_ge(s_ctx0, 3)
            sequences(act, None, sequence)
            act.wait_ge(s_const, 1)
            pad(act, 1)

            def slot_tile(n, a, i, before, after):
                if live(n, FTILES):
                    act.wait_ge(s_hT, n + 1)
                    wait(act, s_down, n - 1)
                    nc.scalar.activation(hT[:, a % 2, :, :], ps_hT[:, :], ACT.Relu).then_inc(s_hTr, 1)
                if live(n - 2, FTILES):
                    b = (a - 2) % RING
                    act.wait_ge(s_yb, n - 1)
                    if live(n - 2 - RING, FTILES):
                        act.wait_ge(s_placed[b], 16 * (i if b == a - 2 else i - 1))
                    nc.scalar.activation(y[:, b, :], y_biased[:, b % 2, :], ACT.Copy,
                                         scale=slot_w[:, b, :]).then_inc(s_yr, 1)
                if live(n + 3, FTILES):
                    act.wait_ge(s_sT, n + 4)
                    wait(act, s_up, n + 2)
                    nc.scalar.activation(sT_hi[:, (a + 1) % 2, :], ps_slot[:, 0:P], ACT.Copy).then_inc(s_sh, 1)

            slot_tiles(act, slot_tile)

            for c in range(TILES // Y_TILES):
                act.wait_ge(s_tot, c + 1)
                act.dma_start(out.rearrange("b s d -> (b s) d")[c * Y_TILES * P:(c + 1) * Y_TILES * P, :]
                              .rearrange("(j p) d -> p j d", p=P),
                              y_first[:, c * Y_TILES:c * Y_TILES + Y_TILES, :]).then_inc(s_out, 16)
            act.wait_ge(s_out, 16 * TILES // Y_TILES)

        @block.vector
        def _(dve):
            step = Steps(dve, s_vec)
            step.done(nc.vector.memset(zeros[:, :], 0.0))
            dve.wait_ge(s_tok, 16)
            step.done(nc.vector.tensor_scalar(other[:, :], tokens[:, :], 39990, None, ALU.is_gt))
            step.done(nc.vector.tensor_tensor_scan(seg_count[:, :], other[:, :], zeros[:, :], 0.0, ALU.add, ALU.add))
            step.done(nc.vector.tensor_scalar(seg_int[:, :], seg_count[:, :], NSEG - 1, None, ALU.bitwise_and))
            nc.vector.tensor_scalar(segments[:, :], seg_int[:, :], float(NNEST), None, ALU.add).then_inc(s_ids, 1)
            step.done(nc.vector.tensor_scalar(delta[:, :], tokens[:, :], 40, None, ALU.is_equal))
            for code in (123, 91):
                step.done(nc.vector.scalar_tensor_tensor(delta[:, :], tokens[:, :], code, delta[:, :],
                                                         ALU.is_equal, ALU.add))
            step.done(nc.vector.tensor_scalar(other[:, :], tokens[:, :], 41, None, ALU.is_equal))
            for code in (125, 93):
                step.done(nc.vector.scalar_tensor_tensor(other[:, :], tokens[:, :], code, other[:, :],
                                                         ALU.is_equal, ALU.add))
            step.done(nc.vector.tensor_tensor(delta[:, :], delta[:, :], other[:, :], ALU.subtract))
            step.done(nc.vector.tensor_tensor_scan(depth[:, :], delta[:, :], zeros[:, :], 0.0, ALU.add, ALU.add))
            step.done(nc.vector.tensor_tensor_scan(floor[:, :], depth[:, :], zeros[:, :], 0.0, ALU.min, ALU.min))
            step.done(nc.vector.tensor_tensor(depth[:, :], depth[:, :], floor[:, :], ALU.subtract))
            nc.vector.tensor_scalar(nesting[:, :], depth[:, :], float(NNEST - 1), 0.0, ALU.min, ALU.max)\
                .then_inc(s_ids, 1)

            dve.wait_ge(s_wT, 1)
            step.done(nc.vector.tensor_copy(pos_part[:, :, :], ps_oy[:, 0:2 * D].rearrange("p (a d) -> p a d", a=2)))
            dve.wait_ge(s_bias_w, 16 * PARTS)
            step.add(nc.vector.tensor_copy(rest_two[:, 0, :], ps_oy[0:TR, 2 * D:3 * D]))
            step.done(nc.vector.tensor_copy(rest_two[:, 1, :], bias_rows[:, :]))
            step.done(nc.vector.tensor_copy(split_hi[:, :, :], rest_two[:, :, :]))
            step.done(nc.vector.tensor_tensor(rest_one[:, :, :], rest_two[:, :, :], split_hi[:, :, :], ALU.subtract))
            step.done(nc.vector.tensor_copy(split_mid[:, :, :], rest_one[:, :, :]))
            step.done(nc.vector.tensor_tensor(rest_two[:, :, :], rest_one[:, :, :], split_mid[:, :, :], ALU.subtract))
            step.done(nc.vector.tensor_copy(split_lo[:, :, :], rest_two[:, :, :]))
            for r, part in enumerate((split_hi, split_mid, split_lo)):
                last = nc.vector.tensor_copy(table[SLOT * r:SLOT * r + SLOT, :, :], part[SLOT * r:SLOT * r + SLOT, :, :])
            last.then_inc(s_wTc, 1)

            def split_weights():
                dve.wait_ge(s_hi, 2)
                nc.vector.tensor_tensor(qkv_lo[:, 2, :], ps_vc[:, :], qkv_hi[:, 2, :].bitcast(f32), ALU.subtract)
                dve.wait_ge(s_hi, 3)
                nc.vector.scalar_tensor_tensor(qkv_lo[:, 0, :], ps_out[:, 0, :], DH ** -0.5, qkv_hi[:, 0, :].bitcast(f32),
                                               ALU.mult, ALU.subtract)
                dve.wait_ge(s_hi, 4)
                nc.vector.tensor_tensor(qkv_lo[:, 1, :], ps_out[:, 1, :], qkv_hi[:, 1, :].bitcast(f32),
                                        ALU.subtract).then_inc(s_wTc, 1)

            def hot(p, a):
                wait(dve, s_emb, p - 1)
                nc.vector.tensor_scalar(one_hot[:, a, :], row_of[:, span(p * S, S)], table_id[:, 0:1], None,
                                        ALU.is_equal).then_inc(s_hot, 1)

            def stats_of(p, st):
                for j in range(2):
                    last = nc.vector.bn_stats(st[:, j, :], h[:, span(2 * p + j, 1), :].rearrange("p o d -> p (o d)"))
                step.add(last)

            def moments_of(a, st, mom, out_sem):
                for j in range(2):
                    last = nc.vector.bn_aggr(mom[:, a, j, :], st[:, j, :])
                last.then_inc(out_sem, 1)

            def embed(p, a):
                dve.wait_ge(s_emb, p + 1)
                nc.vector.tensor_tensor(h[:, span(2 * p, 2), :], ps_ln[:, 0:S].rearrange("p (a d) -> p a d", a=2),
                                        pos_part[:, :, :], ALU.add).then_inc(s_h, 1)

            def xT_low(p, a):
                dve.wait_ge(s_xh, p + 1)
                nc.vector.tensor_tensor(xT_lo[:, a, :], ps_ln[:, 0:S], xT_hi[:, a, :].bitcast(f32),
                                        ALU.subtract).then_inc(s_xl, 1)

            def head_max(t, ps, n, done_sem):
                dve.wait_ge(done_sem, t + 1)
                step.add(nc.vector.tensor_reduce(qk_max[:, n, :], ps[:, :].rearrange("p (h f) -> p h f", h=HEADS),
                                                 AX.X, ALU.max))

            def subtract_max(t, a, ps, dst, n, free_sem, out_sem):
                wait(dve, free_sem, t - 1)
                nc.vector.tensor_tensor(dst[:, a, :].rearrange("p (h f) -> p h f", h=HEADS),
                                        ps[:, :].rearrange("p (h f) -> p h f", h=HEADS),
                                        qk_max[:, n, :, None].to_broadcast([P, HEADS, DH]),
                                        ALU.subtract).then_inc(out_sem, 1)

            heads = ps_out[:, :, 0:HC * (DH + 1)].rearrange("p r (c d) -> p r c d", c=HC)

            def divisor(t):
                dve.wait_ge(s_o, t + 1)
                step.add(nc.vector.tensor_scalar(d_sum[:, :].rearrange("p (r c) -> p r c", r=2), heads[:, :, :, DH],
                                                 D_EPS, None, ALU.add))

            def invert():
                step.add(nc.vector.reciprocal(d_inv[:, :], d_sum[:, :]))

            def divide(t, a):
                nc.vector.tensor_tensor(
                    heads_out[:, a, :].rearrange("p (r c d) -> p r c d", r=2, c=HC), heads[:, :, :, 0:DH],
                    d_inv[:, :].rearrange("p (r c) -> p r c", r=2)[:, :, :, None].to_broadcast([P, 2, HC, DH]),
                    ALU.mult).then_inc(s_or, 1)

            def residual(t):
                dve.wait_ge(s_y, t + 1)
                at = h[:, span(t, 1), :].rearrange("p o d -> p (o d)")
                nc.vector.tensor_tensor(at, ps_oy[:, 0:D], at, ALU.add).then_inc(s_h2, 1)

            def read_logits(p):
                dve.wait_ge(s_lg, p + 1)
                nc.vector.tensor_tensor(logits[:, :, :], ps_ln[:, 0:2 * E].rearrange("p (j e) -> p j e", j=2),
                                        gate_b[:, None, :].to_broadcast([P, 2, E]), ALU.add).then_inc(s_lgr, 1)

            def find_top():
                for j in range(2):
                    last = nc.vector.max(top[:, j, :], logits[:, j, :])
                step.add(last)

            def find_top_ids():
                for j in range(2):
                    last = nc.vector.max_index(top_id[:, j, :], top[:, j, :], logits[:, j, :])
                step.add(last)

            def below_top():
                nc.vector.tensor_tensor(below[:, :, :], top[:, :, :], top[:, :, 0:1].to_broadcast([P, 2, E]),
                                        ALU.subtract).then_inc(s_below, 1)

            def choose(p):
                weighed(dve, p - 1)
                step.done(nc.vector.tensor_tensor(
                    chosen[:, :, :, :], expert_id[:, None, None, :].to_broadcast([P, 2, TOP, E]),
                    top_id[:, :, 0:TOP, None].to_broadcast([P, 2, TOP, E]), ALU.is_equal))
                nc.vector.tensor_tensor(mask[:, :, :], chosen[:, :, 0, :], chosen[:, :, 1, :], ALU.add)\
                    .then_inc(s_mask, 1)

            def read_ranks(p):
                dve.wait_ge(s_rank, p + 1)
                step.add(nc.vector.tensor_tensor(row_at[:, :, :], ps_ln[:, 0:2 * E].rearrange("p (j e) -> p j e", j=2),
                                                 next_row[:, None, :].to_broadcast([P, 2, E]), ALU.add))

            def move_next_row():
                nc.vector.tensor_tensor(next_row[:, :], ps_ln[:, 2 * E:3 * E], next_row[:, :], ALU.add)\
                    .then_inc(s_rankr, 1)

            def rows_of_choices():
                step.add(nc.vector.tensor_tensor(chosen_at[:, :, :, :], chosen[:, :, :, :],
                                                 row_at[:, :, None, :].to_broadcast([P, 2, TOP, E]), ALU.mult))

            def give_rows(p, a):
                nc.vector.tensor_reduce(row_id[:, place_of(p, a), :, :], chosen_at[:, :, :, :], AX.X, ALU.max).then_inc(s_id, 1)

            def even(p, a):
                t = 2 * p
                more = live(t + 1, TILES)
                ranks = live(p - 3)
                if live(t - 2, TILES):
                    residual(t - 2)
                if more:
                    head_max(t + 1, ps_q, 0, s_q)
                if ranks:
                    read_ranks(p - 3)
                if more or ranks:
                    step.wait()
                if more:
                    subtract_max(t + 1, 1, ps_q, q_prime, 0, s_qT, s_qs)
                if ranks:
                    move_next_row()
                    rows_of_choices()
                if more:
                    head_max(t + 1, ps_k, 1, s_k)
                if more or ranks:
                    step.wait()
                if more:
                    subtract_max(t + 1, 1, ps_k, k_prime, 1, s_c, s_ks)
                if ranks:
                    give_rows(p - 3, 1 - a)
                if live(p):
                    divisor(t)
                if live(p + 1):
                    xT_low(p + 1, 1 - a)
                if live(p):
                    step.wait()
                    invert()
                if isinstance(p, int) and p + 2 == HEAD_SEQS:
                    dve.wait_ge(s_row, 16 * PARTS)
                if live(p + 2):
                    hot(p + 2, a)
                if live(p):
                    step.wait()
                    divide(t, 0)

            def odd(p, a):
                t = 2 * p + 1
                more = live(t + 1, TILES)
                if live(t - 2, TILES):
                    residual(t - 2)
                if more:
                    head_max(t + 1, ps_q, 0, s_q)
                if live(p + 2):
                    embed(p + 2, a)
                if more:
                    step.wait()
                if live(p - 1):
                    dve.wait_ge(s_h2, 2 * p)
                if live(p + 2):
                    dve.wait_ge(s_h, p + 3)
                if more:
                    subtract_max(t + 1, 0, ps_q, q_prime, 0, s_qT, s_qs)
                    head_max(t + 1, ps_k, 1, s_k)
                if live(p + 2):
                    stats_of(p + 2, stats)
                if live(p - 1):
                    stats_of(p - 1, stats2)
                if live(p - 2):
                    read_logits(p - 2)
                step.wait()
                if live(p - 2):
                    dve.wait_ge(s_lgr, p - 1)
                if more:
                    subtract_max(t + 1, 0, ps_k, k_prime, 1, s_c, s_ks)
                if live(p + 2):
                    moments_of(a, stats, moments, s_mom)
                if live(p - 1):
                    moments_of(1 - a, stats2, moments2, s_mom2)
                if live(p - 2):
                    find_top()
                if live(p):
                    divisor(t)
                if live(p) or live(p - 2):
                    step.wait()
                if live(p):
                    invert()
                if live(p - 2):
                    find_top_ids()
                    below_top()
                if live(p) or live(p - 2):
                    step.wait()
                if live(p):
                    divide(t, 1)
                if live(p - 2):
                    choose(p - 2)

            def weigh_last(p, a):
                dve.wait_ge(s_exps, p + 1)
                step.done(nc.vector.tensor_reduce(last_denom[:, :], exps[:, :, :], AX.X, ALU.add))
                step.done(nc.vector.scalar_tensor_tensor(last_denom[:, :], last_denom[:, :], TOP_EPS, exps[:, :, 1],
                                                         ALU.mult, ALU.add))
                step.done(nc.vector.tensor_scalar(last_denom[:, :], last_denom[:, :], 1.0, None, ALU.add))
                step.done(nc.vector.reciprocal(last_weight[:, :, 0], last_denom[:, :]))
                step.done(nc.vector.tensor_tensor(last_weight[:, :, 1], last_weight[:, :, 0], exps[:, :, 1], ALU.mult))
                nc.vector.scalar_tensor_tensor(rows[:, place_of(p, a), :, D + E:ROW], chosen[:, :, 1, :], float(B * S),
                                               token_id[:, 2 * p:2 * p + 2, None].to_broadcast([P, 2, E]),
                                               ALU.mult, ALU.add)
                step.done(nc.vector.tensor_tensor(last_chosen_w[:, :, :, :], chosen[:, :, :, :],
                                                  last_weight[:, :, :, None].to_broadcast([P, 2, TOP, E]), ALU.mult))
                nc.vector.tensor_tensor(rows[:, place_of(p, a), :, D:D + E], last_chosen_w[:, :, 0, :], last_chosen_w[:, :, 1, :],
                                        ALU.add).then_inc(s_last_weighed, 1)

            def sequence(p, a, half):
                if isinstance(p, int) and p == -1:
                    split_weights()
                even(p, a)
                odd(p, a)
                if isinstance(p, int) and p - 2 in LAST:
                    weigh_last(p - 2, a)

            dve.wait_ge(s_row_head, 16 * PARTS)
            dve.wait_ge(s_gate_w, 16 * GATE_DMAS)
            dve.wait_ge(s_const, 1)
            sequences(dve, step, sequence, 30)

            nc.vector.tensor_copy(pad_at[:, :], next_row[:, :]).then_inc(s_pad_at, 1)
            step.done(nc.vector.tensor_tensor(rows_used[:, :], next_row[:, :], expert_at[:, 0:E], ALU.subtract))
            step.done(nc.vector.tensor_scalar(rows_up[:, :], rows_used[:, :], float(P - 1), None, ALU.add))
            step.done(nc.vector.tensor_scalar(tiles_of[:, :], rows_up[:, :], P.bit_length() - 1, None,
                                              ALU.logical_shift_right))
            step.add(nc.vector.memset(tile_expert[:, :], 0.0))
            step.done(nc.vector.memset(shift_at[:, :], 0.0))
            step.done(nc.vector.tensor_tensor_scan(tiles_to[:, :], tiles_of[:, :], shift_at[:, 0:E], 0.0, ALU.add, ALU.add))
            step.done(nc.vector.scalar_tensor_tensor(shift_at[:, 1:E + 1], tiles_to[:, :], -float(P), expert_at[:, 1:E + 1],
                                                     ALU.mult, ALU.add))
            step.done(nc.vector.tensor_tensor(shift_by[:, :], shift_at[:, 1:E + 1], shift_at[:, 0:E], ALU.subtract))
            step.done(nc.vector.tensor_tensor(past[:, :, :], tiles_to[:, None, :].to_broadcast([P, FTILES, E]),
                                              tile_id[:, :, None].to_broadcast([P, FTILES, E]), ALU.is_le))
            step.add(nc.vector.tensor_reduce(expert_f[:, :], past[:, :, :], AX.X, ALU.add))
            step.done(nc.vector.tensor_tensor(past_by[:, :, :], past[:, :, :],
                                              shift_by[:, None, :].to_broadcast([P, FTILES, E]), ALU.mult))
            step.done(nc.vector.tensor_reduce(first_f[:, :], past_by[:, :, :], AX.X, ALU.add))
            nc.vector.scalar_tensor_tensor(tile_row[:, :], tile_id[:, :], float(P), first_f[:, :], ALU.mult, ALU.add)
            nc.vector.tensor_scalar(tile_expert[:, 1:FTILES + 1], expert_f[:, :], float(E - 1), None, ALU.min)\
                .then_inc(s_tiles, 1)
            dve.wait_ge(s_tiles, 1)

            def expert_of(d):
                return tile_expert[:, :].rearrange("p (g r) -> p g r", r=RING)\
                    [:, d // RING:d // RING + FTILES // RING, d % RING]

            step.add(nc.vector.tensor_copy(high_digit[:, :], expert_of(DIGITS - 1)))
            step.done(nc.vector.tensor_tensor(
                digits[:, :, :], tile_expert[:, 0:FTILES].rearrange("p (g r) -> p g r", r=RING),
                digit[:, None, :].to_broadcast([P, FTILES // RING, RING]), ALU.mult))
            step.done(nc.vector.tensor_reduce(group_f[:, :], digits[:, :, :], AX.X, ALU.add))
            for d in range(RING, LOW_DIGITS):
                step.done(nc.vector.scalar_tensor_tensor(low_word[:, :] if d == LOW_DIGITS - 1 else group_f[:, :],
                                                         expert_of(d), float(E ** d), group_f[:, :], ALU.mult, ALU.add))
            nc.vector.scalar_tensor_tensor(group_experts[:, :], high_digit[:, :], E_BITS * LOW_DIGITS, low_word[:, :],
                                           ALU.logical_shift_left, ALU.bitwise_or).then_inc(s_groups, 1)
            dve.wait_ge(s_groups, 1)
            dve.wait_ge(s_ffn_w, 16 * (E + 2))

            def slot_tile(n, a, i, before, after):
                if live(n + 3, FTILES):
                    dve.wait_ge(s_sh, n + 4)
                    nc.vector.tensor_tensor(sT_lo[:, (a + 1) % 2, :], ps_slot[:, 0:P],
                                            sT_hi[:, (a + 1) % 2, :].bitcast(f32), ALU.subtract).then_inc(s_sl, 1)
                if live(n + 2, FTILES):
                    dve.wait_ge(s_up, n + 3)
                    wait(dve, s_hT, n + 1)
                    nc.vector.tensor_tensor(hidden[:, a % 2, :], ps_up[a % 2][:, :], b1_all[:, bass.ds(after * FF, FF)],
                                            ALU.add).then_inc(s_hid, 1)
                if live(n + 2, FTILES):
                    b = (a + 2) % RING
                    if live(n + 2 - RING, FTILES):
                        dve.wait_ge(s_placed[b], 16 * (i if b == a + 2 else i + 1))
                    nc.vector.tensor_copy(slot_w[:, b, :], slot_rows[:, b, bass.ds(after + D, 1)])
                    nc.vector.tensor_copy(place[:, b, :], slot_rows[:, b, bass.ds(after + (D + E), 1)])\
                        .then_inc(s_meta, 1)
                if live(n - 1, FTILES):
                    dve.wait_ge(s_down, n)
                    wait(dve, s_yr, n - 2)
                    nc.vector.tensor_tensor(y_biased[:, (a - 1) % 2, :], ps_y[(a - 1) % 2][:, 0:D],
                                            b2_all[:, bass.ds(before * D, D)], ALU.add).then_inc(s_yb, 1)

            slot_tiles(dve, slot_tile, groups=group_experts)

            for c in range(TILES // Y_TILES):
                at = slice(c * Y_TILES, c * Y_TILES + Y_TILES)
                dve.wait_ge(s_back[c], 16 * TOP)
                step.done(nc.vector.tensor_tensor(y_first[:, at, :], y_first[:, at, :], y_second[:, at, :], ALU.add))
                nc.vector.tensor_tensor(y_first[:, at, :], y_first[:, at, :], h[:, at, :], ALU.add).then_inc(s_tot, 1)

        @block.tensor
        def _(pe):
            pe.wait_ge(s_ident, 1)
            pe.wait_ge(s_emb_w, 16 * EMB_DMAS)
            idn = ident[:, :]
            for a in range(2):
                nc.tensor.transpose(ps_q[:, a * P:a * P + P], pos_rows[:, a, :], idn)
            nc.tensor.transpose(ps_q[:, 2 * P:2 * P + TR], nest_rows[:, :], ident[0:TR, 0:TR])
            nc.tensor.transpose(ps_q[:, 2 * P + TR:2 * P + 2 * TR], seg_rows[:, :], ident[0:TR, 0:TR]).then_inc(s_t1, 1)
            pe.wait_ge(s_att_w, 16 * ATT_DMAS)
            nc.tensor.transpose(ps_k[:, 0:P], proj_diag[:, :], idn).then_inc(s_t1, 1)
            for c in range(HC):
                last = nc.tensor.transpose(ps_qT[:, c * P:c * P + P], out_rows[:, c * P:c * P + P], idn)
            last.then_inc(s_t1, 1)
            for c in range(HC):
                last = nc.tensor.transpose(ps_vc[:, c * P:c * P + P], qkv_rows[:, 2 * HC + c, :], idn)
            last.then_inc(s_t1, 1)
            pe.wait_ge(s_t1c, 1)
            for a in range(2):
                nc.tensor.matmul(ps_oy[:, a * D:a * D + D], rows_T[:, a * P:a * P + P], tok_rows[:, 0, :],
                                 start=True, stop=True)
            nc.tensor.matmul(ps_oy[0:TR, 2 * D:3 * D], rows_T[:, 2 * P:2 * P + TR], tok_rows[:, 1, :],
                             start=True, stop=False)
            nc.tensor.matmul(ps_oy[0:TR, 2 * D:3 * D], rows_T[:, 2 * P + TR:2 * P + 2 * TR], tok_rows[:, 2, :],
                             start=False, stop=True).then_inc(s_wT, 1)
            pe.wait_ge(s_t1c, 2)
            for n in range(2):
                for c in range(HC):
                    last = nc.tensor.matmul(ps_out[:, n, c * P:c * P + P], qkv_rows[:, n * HC + c, :], proj_T[:, :],
                                            start=True, stop=True)
                last.then_inc(s_wT, 1)
            pe.wait_ge(s_wTc, 1)
            pe.wait_ge(s_const, 1)
            pe.wait_ge(s_gate_w, 16 * GATE_DMAS)

            def warm_up(count, ps):
                for _ in range(count):
                    nc.tensor.matmul(ps, part_ones[:, :], row_of[:, 0:HD], start=True, stop=True)

            def embed(p, a):
                pe.wait_ge(s_hot, p + 1)
                wait(pe, s_x2Tr, p - 3)
                for j in range(2):
                    last = nc.tensor.matmul(ps_ln[:, j * D:j * D + D], one_hot[:, a, j * P:j * P + P], table[:, 0, :],
                                            start=True, stop=True)
                last.then_inc(s_emb, 1)

            def x_transpose(p, a):
                pe.wait_ge(s_xhat, p + 1)
                if live(p - 4):
                    pe.wait_ge(s_rankr, p - 3)
                else:
                    pe.wait_ge(s_h, p + 1)
                for j in range(2):
                    last = nc.tensor.transpose(ps_ln[:, j * P:j * P + P], xhat[:, a, j, :], idn)
                last.then_inc(s_xT, 1)

            def product(n, ps, a, j, out_sem):
                for m, (w, xt) in enumerate(((qkv_hi, xT_hi), (qkv_lo, xT_hi), (qkv_hi, xT_lo))):
                    last = nc.tensor.matmul(ps[:, :], xt[:, a, j * P:j * P + P], w[:, n, :], start=(m == 0), stop=(m == 2))
                last.then_inc(out_sem, 1)

            def q_product(t, p, a, j):
                pe.wait_ge(s_xl, p + 1)
                wait(pe, s_qs, t)
                product(0, ps_q, a, j, s_q)

            def k_product(t, a, j):
                wait(pe, s_ks, t)
                product(1, ps_k, a, j, s_k)

            def v_product(t, a, j):
                wait(pe, s_cr, t)
                product(2, ps_vc, a, j, s_v)

            def q_transpose(t, a):
                pe.wait_ge(s_qp, t + 1)
                wait(pe, s_qTr, t)
                for c in range(HC):
                    last = nc.tensor.transpose(ps_qT[:, c * P:c * P + P], q_prime[:, a, c * P:c * P + P], idn)
                last.then_inc(s_qT, 1)

            def context_product(t, a):
                pe.wait_ge(s_kp, t + 1)
                pe.wait_ge(s_vo, t + 1)
                for n in range(HEADS):
                    r = DH * (n % 2)
                    last = nc.tensor.matmul(ps_ctx[r:r + DH, n // 2, :], k_prime[:, a, n * DH:n * DH + DH],
                                            v_ones[:, a, n, :], start=True, stop=True)
                last.then_inc(s_c, 1)

            def out_product(t, a):
                pe.wait_ge(s_cr, t + 1)
                pe.wait_ge(s_qTr, t + 1)
                wait(pe, s_or, t)
                for c in range(HC):
                    at = c % 2 * 2 * (DH + 1)
                    last = nc.tensor.matmul(ps_out[:, c // 2, at:at + 2 * (DH + 1)], qT[:, a, c, :],
                                            context[:, a, c, :, :].rearrange("p r d -> p (r d)"), start=True, stop=True)
                last.then_inc(s_o, 1)

            def o_transpose(t, a):
                pe.wait_ge(s_or, t + 1)
                wait(pe, s_h2, t)
                for c in range(HC):
                    last = nc.tensor.transpose(ps_oy[:, c * P:c * P + P], heads_out[:, a, c * P:c * P + P], idn)
                last.then_inc(s_oT, 1)

            def y_product(t, a):
                pe.wait_ge(s_oTr, t + 1)
                nc.tensor.matmul(ps_oy[:, 0:D], part_ones[:, :], table[:, 1, :], start=True, stop=False)
                for c in range(HC):
                    last = nc.tensor.matmul(ps_oy[:, 0:D], oT[:, a, c, :], out_w[:, c, :], start=False, stop=(c == HC - 1))
                last.then_inc(s_y, 1)

            def x2_transpose(p, a):
                pe.wait_ge(s_xhat2, p + 1)
                if live(p + 3):
                    pe.wait_ge(s_xl, p + 4)
                else:
                    pe.wait_ge(s_rankr, p)
                for j in range(2):
                    last = nc.tensor.transpose(ps_ln[:, j * P:j * P + P], rows[:, place_of(p, a), j, 0:D], idn)
                last.then_inc(s_x2T, 1)

            def gate_product(p, a):
                pe.wait_ge(s_x2Tr, p + 1)
                if live(p + 4):
                    pe.wait_ge(s_h, p + 5)
                for j in range(2):
                    last = nc.tensor.matmul(ps_ln[:, j * E:j * E + E], x2T[:, a, j * P:j * P + P], gate_w[:, :],
                                            start=True, stop=True)
                last.then_inc(s_lg, 1)

            def rank_product(p):
                pe.wait_ge(s_mask, p + 1)
                nc.tensor.matmul(ps_ln[:, 0:E], before[:, :], mask[:, 0, :], start=True, stop=True)
                nc.tensor.matmul(ps_ln[:, E:2 * E], before[:, :], mask[:, 1, :], start=True, stop=False)
                nc.tensor.matmul(ps_ln[:, E:2 * E], ones[:, :], mask[:, 0, :], start=False, stop=True)
                nc.tensor.matmul(ps_ln[:, 2 * E:3 * E], ones[:, :], mask[:, 0, :], start=True, stop=False)
                nc.tensor.matmul(ps_ln[:, 2 * E:3 * E], ones[:, :], mask[:, 1, :], start=False, stop=True)\
                    .then_inc(s_rank, 1)

            def sequence(p, a, half):
                for j in range(2):
                    t = 2 * p + j
                    np_, na, nj = (p, a, 1) if j == 0 else (p + 1, 1 - a, 0)
                    more = live(t + 1, TILES)
                    if isinstance(t, int) and t == -2:
                        warm_up(9, ps_k[:, :])
                    if isinstance(t, int) and t == -1:
                        pe.wait_ge(s_wTc, 2)
                        pe.wait_ge(s_hi, 4)
                    if more:
                        q_product(t + 1, np_, na, nj)
                    if j == 1 and live(p + 2):
                        embed(p + 2, a)
                    if live(p):
                        context_product(t, j)
                    if j == 0 and live(p - 3):
                        rank_product(p - 3)
                    if live(t - 1, TILES):
                        o_transpose(t - 1, 1 - j)
                    if more:
                        k_product(t + 1, na, nj)
                    if j == 1 and live(p - 2):
                        gate_product(p - 2, a)
                    if live(p):
                        out_product(t, j)
                    if j == 0 and live(p + 1):
                        x_transpose(p + 1, 1 - a)
                    if more:
                        v_product(t + 1, na, nj)
                        q_transpose(t + 1, 1 - j)
                    if live(t - 1, TILES):
                        y_product(t - 1, 1 - j)
                    if j == 0 and live(p - 2):
                        x2_transpose(p - 2, a)

            sequences(pe, None, sequence)


            pe.wait_ge(s_groups, 1)
            warm_up(12, ps_out[:, 0, :])
            pe.wait_ge(s_w1l, SEQS)
            pe.wait_ge(s_ffn_w, 16 * (E + 2))

            def slot_tile(n, a, i, before, after):
                if live(n, FTILES):
                    pe.wait_ge(s_hid, n + 1)
                    wait(pe, s_hTr, n)
                    for c in range(FC):
                        last = nc.tensor.transpose(ps_hT[:, c * P:c * P + P], hidden[:, a % 2, c * P:c * P + P], idn)
                    last.then_inc(s_hT, 1)
                if live(n + 2, FTILES):
                    pe.wait_ge(s_sl, n + 3)
                    wait(pe, s_hid, n + 1)
                    for m, (w, st) in enumerate(((w1_hi, sT_hi), (w1_lo, sT_hi), (w1_hi, sT_lo))):
                        last = nc.tensor.matmul(ps_up[a % 2][:, :], st[:, a % 2, :], w[:, bass.ds(after * FF, FF)],
                                                start=(m == 0), stop=(m == 2))
                    last.then_inc(s_up, 1)
                if live(n + 3, FTILES):
                    b = (a + 3) % RING
                    pe.wait_ge(s_slot[b], 16 * (i + 1 if b == a + 3 else i + 2))
                    wait(pe, s_sl, n + 3)
                    nc.tensor.transpose(ps_slot[:, 0:P], slot_rows[:, b, 0:D], idn).then_inc(s_sT, 1)
                if isinstance(n, int) and n < 0:
                    warm_up(4, ps_out[:, 0, :])
                if live(n - 1, FTILES):
                    b = (a - 1) % 2
                    pe.wait_ge(s_hTr, n)
                    wait(pe, s_yb, n - 2)
                    for c in range(FC):
                        last = nc.tensor.matmul(ps_y[b][:, 0:D], hT[:, b, c, :],
                                                w2_all[:, c, :, :].rearrange("p e d -> p (e d)")
                                                [:, bass.ds(before * D, D)],
                                                start=(c == 0), stop=(c == FC - 1))
                    last.then_inc(s_down, 1)

            slot_tiles(pe, slot_tile, groups=group_experts)


_INS = ['x', 'L0_tok_pos_table', 'L0_tok_nest_table', 'L0_tok_seg_table', 'L0_tok_W', 'L0_attn_w_qkv',
        'L0_attn_w_out', 'L0_attn_b_out', 'L0_attn_proj', 'L0_ffn_Wg', 'L0_ffn_bg', 'L0_ffn_W1', 'L0_ffn_b1',
        'L0_ffn_W2', 'L0_ffn_b2']
_OUT = (16, 256, 128)


def kernel(**inputs):
    import numpy as _np
    import concourse.bacc as _bacc
    from concourse import mybir as _mybir
    from concourse.bass_utils import run_bass_kernel_spmd as _run

    nc = _bacc.Bacc("TRN2", target_bir_lowering=False, num_devices=1)
    arrays, args = {}, []
    for name in _INS:
        a = _np.ascontiguousarray(inputs[name])
        arrays[f"in_{name}"] = a
        args.append(nc.dram_tensor(f"in_{name}", a.shape, _mybir.dt.from_np(a.dtype), kind="ExternalInput").ap())
    args.append(nc.dram_tensor("out", _OUT, _mybir.dt.float32, kind="ExternalOutput").ap())
    lm_tower_kernel(nc, *args)
    r = _run(nc, [arrays], core_ids=[0])
    return r.results[0]["out"]
```
